# Optimizing a Trainium2 kernel written in Bass

```python
import numpy as np
import jax
import jax.numpy as jnp

def _softmax(x, axis=-1):
    return jax.nn.softmax(x, axis=axis)

def _gelu(x):
    return jax.nn.gelu(x, approximate=True)

def _silu(x):
    return jax.nn.silu(x)

def _sigmoid(x):
    return jax.nn.sigmoid(x)

def _layernorm(x, axis=-1, eps=1e-05):
    m = jnp.mean(x, axis=axis, keepdims=True)
    v = jnp.var(x, axis=axis, keepdims=True)
    return (x - m) / jnp.sqrt(v + eps)

def _scatter_add(tgt, idx, src, axis=0):
    return tgt.at[idx].add(src)

def _segment_sum(src, seg, n):
    return jax.ops.segment_sum(src, seg, n)
kernel_name = 'mk_xattn_seq_d4_seqx_r8_2963e8'

def setup_inputs(seed: int=0):
    np.random.seed(seed)
    _w = jnp.asarray

    def _rec_inputs():
        import jax
        import jax.numpy as jnp
        _rk = jax.random.key(seed)
        x = 7.22e-05 + 1 * jax.random.normal(jax.random.fold_in(_rk, 1), (4, 256, 256), jnp.float32)
        _lenS = 256 - jax.random.randint(jax.random.fold_in(_rk, 7), (4,), 0, max(1, 256 // 4) + 1, jnp.int32)
        _lenS2 = 256 - jax.random.randint(jax.random.fold_in(_rk, 8), (4,), 0, max(1, 256 // 4) + 1, jnp.int32)
        _ctx_2048P = jax.random.normal(jax.random.fold_in(_rk, 11), (4, 16, 256), jnp.float32)
        _ctx_2048c = jax.random.dirichlet(jax.random.fold_in(_rk, 511), 0.3 * jnp.ones((16,), jnp.float32), (4, 256))
        _ctx_2048t = jnp.einsum('bsk,bkd->bsd', _ctx_2048c, _ctx_2048P)
        _ctx_2048t = _ctx_2048t * jax.lax.rsqrt(jnp.mean(jnp.square(_ctx_2048t)) + 1e-12) * 0.953939
        ctx_2048 = 4.13588e-05 + 0.999923 * (_ctx_2048t + 0.3 * jax.random.normal(jax.random.fold_in(_rk, 611), (4, 256, 256), jnp.float32))
        _validS = jnp.arange(256)[None, :] < _lenS[:, None]
        _validS2 = jnp.arange(256)[None, :] < _lenS2[:, None]
        _causal = jnp.tril(jnp.ones((256, 256), dtype=bool))
        mask_Bx1xSxS2_ff0 = jnp.where(jnp.ones((4, 1, 256, 256), dtype=bool), 0.0, -1000000000.0).astype(jnp.float32)
        mask_1x1xSxS2_fc1 = jnp.where(jnp.broadcast_to(_validS2[0:1, None, None, :], (1, 1, 256, 256)), 1.0, 0.0).astype(jnp.float32)
        mask_Bx1xSxS2_ff1 = jnp.where(jnp.ones((4, 1, 256, 256), dtype=bool), 1.0, 0.0).astype(jnp.float32)
        return (x, ctx_2048, mask_Bx1xSxS2_ff0, mask_1x1xSxS2_fc1, mask_Bx1xSxS2_ff1)
    x, ctx_2048, mask_Bx1xSxS2_ff0, mask_1x1xSxS2_fc1, mask_Bx1xSxS2_ff1 = _rec_inputs()

    def _L0_xattn_setup():
        import jax, jax.numpy as jnp
        import numpy as np
        H = 256
        NH = 32
        KVH = 8
        HD = H // NH
        GROUPS = NH // KVH
        EPS = 1e-06
        B, L, S = (4, 128, 128)

        def _gqa_forward(hidden_state, encoder_hidden_state, encoder_attention_mask, Wq, bq, Wk, bk, Wv, bv, Wo, bo, gamma, beta):
            b, l, _ = hidden_state.shape
            s = encoder_hidden_state.shape[1]
            q = hidden_state @ Wq + bq
            k = encoder_hidden_state @ Wk + bk
            v = encoder_hidden_state @ Wv + bv
            q = q.reshape(b, l, KVH, GROUPS, HD).transpose(0, 2, 3, 1, 4)
            k = k.reshape(b, s, KVH, HD).transpose(0, 2, 1, 3)
            v = v.reshape(b, s, KVH, HD).transpose(0, 2, 1, 3)
            scale = 1.0 / jnp.sqrt(jnp.asarray(HD, q.dtype))
            scores = jnp.einsum('bkgld,bksd->bkgls', q, k) * scale
            scores = scores + encoder_attention_mask[:, :, None, :, :]
            attn = jax.nn.softmax(scores, axis=-1)
            out = jnp.einsum('bkgls,bksd->bkgld', attn, v)
            out = out.transpose(0, 3, 1, 2, 4).reshape(b, l, H)
            out = out @ Wo + bo
            x = out + hidden_state
            mu = jnp.mean(x, axis=-1, keepdims=True)
            var = jnp.var(x, axis=-1, keepdims=True)
            return (x - mu) * jax.lax.rsqrt(var + EPS) * gamma + beta
        key = jax.random.key(seed)
        ks = jax.random.split(key, 12)
        sd = 0.02
        return {'hidden_state': jax.random.normal(ks[0], (B, L, H), jnp.float32), 'encoder_hidden_state': jax.random.normal(ks[1], (B, S, H), jnp.float32), 'encoder_attention_mask': jnp.zeros((B, 1, L, S), jnp.float32), 'Wq': jax.random.normal(ks[2], (H, H), jnp.float32) * sd, 'bq': jnp.zeros((H,), jnp.float32), 'Wk': jax.random.normal(ks[3], (H, KVH * HD), jnp.float32) * sd, 'bk': jnp.zeros((KVH * HD,), jnp.float32), 'Wv': jax.random.normal(ks[4], (H, KVH * HD), jnp.float32) * sd, 'bv': jnp.zeros((KVH * HD,), jnp.float32), 'Wo': jax.random.normal(ks[5], (H, H), jnp.float32) * sd, 'bo': jnp.zeros((H,), jnp.float32), 'gamma': jnp.ones((H,), jnp.float32), 'beta': jnp.zeros((H,), jnp.float32)}
    _L0_xattn_all = _L0_xattn_setup()
    _L0_xattn_in = {k: v for k, v in _L0_xattn_all.items() if k in ('Wq', 'bq', 'Wk', 'bk', 'Wv', 'bv', 'Wo', 'bo', 'gamma', 'beta')}
    del _L0_xattn_all

    def _L1_xattn_setup():
        import jax, jax.numpy as jnp
        import numpy as np
        H = 256
        NH = 16
        HD = H // NH
        EPS = 1e-05

        def gelu(x):
            return 0.5 * x * (1.0 + jnp.tanh(0.7978845608028654 * x * (1.0 + 0.044715 * x * x)))

        def layernorm(x, scale, bias):
            m = jnp.mean(x, axis=-1, keepdims=True)
            v = jnp.mean(jnp.square(x - m), axis=-1, keepdims=True)
            return (x - m) * jax.lax.rsqrt(v + EPS) * scale + bias

        def split_heads(x):
            b, s, _ = x.shape
            return x.reshape(b, s, NH, HD).transpose(0, 2, 1, 3)

        def merge_heads(x):
            b, nh, s, hd = x.shape
            return x.transpose(0, 2, 1, 3).reshape(b, s, nh * hd)

        def attention(q, k, v, mask):
            scores = jnp.einsum('bhqd,bhkd->bhqk', q, k) / jnp.sqrt(jnp.float32(HD))
            scores = scores * mask - 10000.0 * (1.0 - mask)
            probs = jax.nn.softmax(scores, axis=-1)
            return jnp.einsum('bhqk,bhkd->bhqd', probs, v)
        key = jax.random.key(seed)
        ks = jax.random.split(key, 16)
        b, s, t = (2, 128, 128)
        w = lambda k, i, o: jax.random.normal(k, (i, o), jnp.float32) * 0.02
        inp = {'hidden_states': jax.random.normal(ks[0], (b, s, H), jnp.float32), 'encoder_states': jax.random.normal(ks[1], (b, t, H), jnp.float32), 'ltor_mask': jnp.tril(jnp.ones((1, 1, s, s), jnp.float32)), 'cross_mask': jnp.ones((b, 1, s, t), jnp.float32), 'ln1_s': jnp.ones((H,), jnp.float32), 'ln1_b': jnp.zeros((H,), jnp.float32), 'w_qkv': w(ks[2], H, 3 * H), 'b_qkv': jnp.zeros((3 * H,), jnp.float32), 'w_ao': w(ks[3], H, H), 'b_ao': jnp.zeros((H,), jnp.float32), 'ln2_s': jnp.ones((H,), jnp.float32), 'ln2_b': jnp.zeros((H,), jnp.float32), 'w_q': w(ks[4], H, H), 'b_q': jnp.zeros((H,), jnp.float32), 'w_kv': w(ks[5], H, 2 * H), 'b_kv': jnp.zeros((2 * H,), jnp.float32), 'w_co': w(ks[6], H, H), 'b_co': jnp.zeros((H,), jnp.float32), 'ln3_s': jnp.ones((H,), jnp.float32), 'ln3_b': jnp.zeros((H,), jnp.float32), 'w1': w(ks[7], H, 4 * H), 'b1': jnp.zeros((4 * H,), jnp.float32), 'w2': w(ks[8], 4 * H, H), 'b2': jnp.zeros((H,), jnp.float32)}
        return inp
    _L1_xattn_all = _L1_xattn_setup()
    _L1_xattn_in = {k: v for k, v in _L1_xattn_all.items() if k in ('ln1_s', 'ln1_b', 'w_qkv', 'b_qkv', 'w_ao', 'b_ao', 'ln2_s', 'ln2_b', 'w_q', 'b_q', 'w_kv', 'b_kv', 'w_co', 'b_co', 'ln3_s', 'ln3_b', 'w1', 'b1', 'w2', 'b2')}
    del _L1_xattn_all

    def _L2_xattn_setup():
        import jax, jax.numpy as jnp
        import numpy as np
        B, Q, S1, S2 = (4, 32, 256, 256)
        D, H, K, F = (256, 16, 128, 1024)
        LN_EPS = 1e-05

        def _layer_norm(x, scale, offset):
            mu = jnp.mean(x, axis=-1, keepdims=True)
            var = jnp.var(x, axis=-1, keepdims=True)
            return (x - mu) * jax.lax.rsqrt(var + LN_EPS) * scale + offset

        def _cross_attention(q_in, kv_in, wq, bq, wk, bk, wv, bv, wo, bo, bias_k, bias_v):
            b, q_len, _ = q_in.shape
            t = kv_in.shape[1]
            qh = (q_in @ wq + bq).reshape(b, q_len, H, K)
            kh = (kv_in @ wk + bk).reshape(b, t, H, K)
            vh = (kv_in @ wv + bv).reshape(b, t, H, K)
            kh = jnp.concatenate([kh, jnp.broadcast_to(bias_k, (b, 1, H, K))], axis=1)
            vh = jnp.concatenate([vh, jnp.broadcast_to(bias_v, (b, 1, H, K))], axis=1)
            scale = jnp.sqrt(jnp.asarray(K, q_in.dtype))
            logits = jnp.einsum('bqhk,bthk->bhqt', qh, kh) / scale
            weights = jax.nn.softmax(logits, axis=-1)
            ctx = jnp.einsum('bhqt,bthk->bqhk', weights, vh).reshape(b, q_len, H * K)
            return ctx @ wo + bo

        def _forward(x, xf_1, xf_2, ln1_scale, ln1_offset, wq1, bq1, wk1, bk1, wv1, bv1, wo1, bo1, bias_k1, bias_v1, ln2_scale, ln2_offset, wq2, bq2, wk2, bk2, wv2, bv2, wo2, bo2, bias_k2, bias_v2, ln_mlp_scale, ln_mlp_offset, w_fc1, b_fc1, w_fc2, b_fc2):
            res = x
            h = _layer_norm(x, ln1_scale, ln1_offset)
            x = res + _cross_attention(h, xf_1, wq1, bq1, wk1, bk1, wv1, bv1, wo1, bo1, bias_k1, bias_v1)
            res = x
            h = _layer_norm(x, ln2_scale, ln2_offset)
            x = res + _cross_attention(h, xf_2, wq2, bq2, wk2, bk2, wv2, bv2, wo2, bo2, bias_k2, bias_v2)
            h = _layer_norm(x, ln_mlp_scale, ln_mlp_offset)
            h = jax.nn.gelu(h @ w_fc1 + b_fc1, approximate=False) @ w_fc2 + b_fc2
            return x + h
        key = jax.random.key(seed)
        ks = iter(jax.random.split(key, 64))

        def rn(shape, s=0.02):
            return jax.random.normal(next(ks), shape, jnp.float32) * s
        inp = {'x': rn((B, Q, D), 1.0), 'xf_1': rn((B, S1, D), 1.0), 'xf_2': rn((B, S2, D), 1.0)}
        for i in (1, 2):
            inp[f'ln{i}_scale'] = jnp.ones((D,), jnp.float32)
            inp[f'ln{i}_offset'] = jnp.zeros((D,), jnp.float32)
            inp[f'wq{i}'] = rn((D, H * K))
            inp[f'bq{i}'] = jnp.zeros((H * K,), jnp.float32)
            inp[f'wk{i}'] = rn((D, H * K))
            inp[f'bk{i}'] = jnp.zeros((H * K,), jnp.float32)
            inp[f'wv{i}'] = rn((D, H * K))
            inp[f'bv{i}'] = jnp.zeros((H * K,), jnp.float32)
            inp[f'wo{i}'] = rn((H * K, D))
            inp[f'bo{i}'] = jnp.zeros((D,), jnp.float32)
            inp[f'bias_k{i}'] = rn((1, 1, H, K))
            inp[f'bias_v{i}'] = rn((1, 1, H, K))
        inp['ln_mlp_scale'] = jnp.ones((D,), jnp.float32)
        inp['ln_mlp_offset'] = jnp.zeros((D,), jnp.float32)
        inp['w_fc1'] = rn((D, F))
        inp['b_fc1'] = jnp.zeros((F,), jnp.float32)
        inp['w_fc2'] = rn((F, D))
        inp['b_fc2'] = jnp.zeros((D,), jnp.float32)
        return inp
    _L2_xattn_all = _L2_xattn_setup()
    _L2_xattn_in = {k: v for k, v in _L2_xattn_all.items() if k in ('ln1_scale', 'ln1_offset', 'wq1', 'bq1', 'wk1', 'bk1', 'wv1', 'bv1', 'wo1', 'bo1', 'bias_k1', 'bias_v1', 'ln2_scale', 'ln2_offset', 'wq2', 'bq2', 'wk2', 'bk2', 'wv2', 'bv2', 'wo2', 'bo2', 'bias_k2', 'bias_v2', 'ln_mlp_scale', 'ln_mlp_offset', 'w_fc1', 'b_fc1', 'w_fc2', 'b_fc2')}
    del _L2_xattn_all

    def _L3_xattn_setup():
        import jax, jax.numpy as jnp
        import numpy as np
        B, Q, S1, S2 = (4, 32, 256, 256)
        D, H, K, F = (256, 16, 128, 1024)
        LN_EPS = 1e-05

        def _layer_norm(x, scale, offset):
            mu = jnp.mean(x, axis=-1, keepdims=True)
            var = jnp.var(x, axis=-1, keepdims=True)
            return (x - mu) * jax.lax.rsqrt(var + LN_EPS) * scale + offset

        def _cross_attention(q_in, kv_in, wq, bq, wk, bk, wv, bv, wo, bo, bias_k, bias_v):
            b, q_len, _ = q_in.shape
            t = kv_in.shape[1]
            qh = (q_in @ wq + bq).reshape(b, q_len, H, K)
            kh = (kv_in @ wk + bk).reshape(b, t, H, K)
            vh = (kv_in @ wv + bv).reshape(b, t, H, K)
            kh = jnp.concatenate([kh, jnp.broadcast_to(bias_k, (b, 1, H, K))], axis=1)
            vh = jnp.concatenate([vh, jnp.broadcast_to(bias_v, (b, 1, H, K))], axis=1)
            scale = jnp.sqrt(jnp.asarray(K, q_in.dtype))
            logits = jnp.einsum('bqhk,bthk->bhqt', qh, kh) / scale
            weights = jax.nn.softmax(logits, axis=-1)
            ctx = jnp.einsum('bhqt,bthk->bqhk', weights, vh).reshape(b, q_len, H * K)
            return ctx @ wo + bo

        def _forward(x, xf_1, xf_2, ln1_scale, ln1_offset, wq1, bq1, wk1, bk1, wv1, bv1, wo1, bo1, bias_k1, bias_v1, ln2_scale, ln2_offset, wq2, bq2, wk2, bk2, wv2, bv2, wo2, bo2, bias_k2, bias_v2, ln_mlp_scale, ln_mlp_offset, w_fc1, b_fc1, w_fc2, b_fc2):
            res = x
            h = _layer_norm(x, ln1_scale, ln1_offset)
            x = res + _cross_attention(h, xf_1, wq1, bq1, wk1, bk1, wv1, bv1, wo1, bo1, bias_k1, bias_v1)
            res = x
            h = _layer_norm(x, ln2_scale, ln2_offset)
            x = res + _cross_attention(h, xf_2, wq2, bq2, wk2, bk2, wv2, bv2, wo2, bo2, bias_k2, bias_v2)
            h = _layer_norm(x, ln_mlp_scale, ln_mlp_offset)
            h = jax.nn.gelu(h @ w_fc1 + b_fc1, approximate=False) @ w_fc2 + b_fc2
            return x + h
        key = jax.random.key(seed)
        ks = iter(jax.random.split(key, 64))

        def rn(shape, s=0.02):
            return jax.random.normal(next(ks), shape, jnp.float32) * s
        inp = {'x': rn((B, Q, D), 1.0), 'xf_1': rn((B, S1, D), 1.0), 'xf_2': rn((B, S2, D), 1.0)}
        for i in (1, 2):
            inp[f'ln{i}_scale'] = jnp.ones((D,), jnp.float32)
            inp[f'ln{i}_offset'] = jnp.zeros((D,), jnp.float32)
            inp[f'wq{i}'] = rn((D, H * K))
            inp[f'bq{i}'] = jnp.zeros((H * K,), jnp.float32)
            inp[f'wk{i}'] = rn((D, H * K))
            inp[f'bk{i}'] = jnp.zeros((H * K,), jnp.float32)
            inp[f'wv{i}'] = rn((D, H * K))
            inp[f'bv{i}'] = jnp.zeros((H * K,), jnp.float32)
            inp[f'wo{i}'] = rn((H * K, D))
            inp[f'bo{i}'] = jnp.zeros((D,), jnp.float32)
            inp[f'bias_k{i}'] = rn((1, 1, H, K))
            inp[f'bias_v{i}'] = rn((1, 1, H, K))
        inp['ln_mlp_scale'] = jnp.ones((D,), jnp.float32)
        inp['ln_mlp_offset'] = jnp.zeros((D,), jnp.float32)
        inp['w_fc1'] = rn((D, F))
        inp['b_fc1'] = jnp.zeros((F,), jnp.float32)
        inp['w_fc2'] = rn((F, D))
        inp['b_fc2'] = jnp.zeros((D,), jnp.float32)
        return inp
    _L3_xattn_all = _L3_xattn_setup()
    _L3_xattn_in = {k: v for k, v in _L3_xattn_all.items() if k in ('ln1_scale', 'ln1_offset', 'wq1', 'bq1', 'wk1', 'bk1', 'wv1', 'bv1', 'wo1', 'bo1', 'bias_k1', 'bias_v1', 'ln2_scale', 'ln2_offset', 'wq2', 'bq2', 'wk2', 'bk2', 'wv2', 'bv2', 'wo2', 'bo2', 'bias_k2', 'bias_v2', 'ln_mlp_scale', 'ln_mlp_offset', 'w_fc1', 'b_fc1', 'w_fc2', 'b_fc2')}
    del _L3_xattn_all
    return {'x': x, 'ctx_2048': ctx_2048, 'mask_Bx1xSxS2_ff0': mask_Bx1xSxS2_ff0, 'mask_1x1xSxS2_fc1': mask_1x1xSxS2_fc1, 'mask_Bx1xSxS2_ff1': mask_Bx1xSxS2_ff1, 'L0_xattn_Wq': _L0_xattn_in['Wq'], 'L0_xattn_bq': _L0_xattn_in['bq'], 'L0_xattn_Wk': _L0_xattn_in['Wk'], 'L0_xattn_bk': _L0_xattn_in['bk'], 'L0_xattn_Wv': _L0_xattn_in['Wv'], 'L0_xattn_bv': _L0_xattn_in['bv'], 'L0_xattn_Wo': _L0_xattn_in['Wo'], 'L0_xattn_bo': _L0_xattn_in['bo'], 'L0_xattn_gamma': _L0_xattn_in['gamma'], 'L0_xattn_beta': _L0_xattn_in['beta'], 'L1_xattn_ln1_s': _L1_xattn_in['ln1_s'], 'L1_xattn_ln1_b': _L1_xattn_in['ln1_b'], 'L1_xattn_w_qkv': _L1_xattn_in['w_qkv'], 'L1_xattn_b_qkv': _L1_xattn_in['b_qkv'], 'L1_xattn_w_ao': _L1_xattn_in['w_ao'], 'L1_xattn_b_ao': _L1_xattn_in['b_ao'], 'L1_xattn_ln2_s': _L1_xattn_in['ln2_s'], 'L1_xattn_ln2_b': _L1_xattn_in['ln2_b'], 'L1_xattn_w_q': _L1_xattn_in['w_q'], 'L1_xattn_b_q': _L1_xattn_in['b_q'], 'L1_xattn_w_kv': _L1_xattn_in['w_kv'], 'L1_xattn_b_kv': _L1_xattn_in['b_kv'], 'L1_xattn_w_co': _L1_xattn_in['w_co'], 'L1_xattn_b_co': _L1_xattn_in['b_co'], 'L1_xattn_ln3_s': _L1_xattn_in['ln3_s'], 'L1_xattn_ln3_b': _L1_xattn_in['ln3_b'], 'L1_xattn_w1': _L1_xattn_in['w1'], 'L1_xattn_b1': _L1_xattn_in['b1'], 'L1_xattn_w2': _L1_xattn_in['w2'], 'L1_xattn_b2': _L1_xattn_in['b2'], 'L2_xattn_ln1_scale': _L2_xattn_in['ln1_scale'], 'L2_xattn_ln1_offset': _L2_xattn_in['ln1_offset'], 'L2_xattn_wq1': _L2_xattn_in['wq1'], 'L2_xattn_bq1': _L2_xattn_in['bq1'], 'L2_xattn_wk1': _L2_xattn_in['wk1'], 'L2_xattn_bk1': _L2_xattn_in['bk1'], 'L2_xattn_wv1': _L2_xattn_in['wv1'], 'L2_xattn_bv1': _L2_xattn_in['bv1'], 'L2_xattn_wo1': _L2_xattn_in['wo1'], 'L2_xattn_bo1': _L2_xattn_in['bo1'], 'L2_xattn_bias_k1': _L2_xattn_in['bias_k1'], 'L2_xattn_bias_v1': _L2_xattn_in['bias_v1'], 'L2_xattn_ln2_scale': _L2_xattn_in['ln2_scale'], 'L2_xattn_ln2_offset': _L2_xattn_in['ln2_offset'], 'L2_xattn_wq2': _L2_xattn_in['wq2'], 'L2_xattn_bq2': _L2_xattn_in['bq2'], 'L2_xattn_wk2': _L2_xattn_in['wk2'], 'L2_xattn_bk2': _L2_xattn_in['bk2'], 'L2_xattn_wv2': _L2_xattn_in['wv2'], 'L2_xattn_bv2': _L2_xattn_in['bv2'], 'L2_xattn_wo2': _L2_xattn_in['wo2'], 'L2_xattn_bo2': _L2_xattn_in['bo2'], 'L2_xattn_bias_k2': _L2_xattn_in['bias_k2'], 'L2_xattn_bias_v2': _L2_xattn_in['bias_v2'], 'L2_xattn_ln_mlp_scale': _L2_xattn_in['ln_mlp_scale'], 'L2_xattn_ln_mlp_offset': _L2_xattn_in['ln_mlp_offset'], 'L2_xattn_w_fc1': _L2_xattn_in['w_fc1'], 'L2_xattn_b_fc1': _L2_xattn_in['b_fc1'], 'L2_xattn_w_fc2': _L2_xattn_in['w_fc2'], 'L2_xattn_b_fc2': _L2_xattn_in['b_fc2'], 'L3_xattn_ln1_scale': _L3_xattn_in['ln1_scale'], 'L3_xattn_ln1_offset': _L3_xattn_in['ln1_offset'], 'L3_xattn_wq1': _L3_xattn_in['wq1'], 'L3_xattn_bq1': _L3_xattn_in['bq1'], 'L3_xattn_wk1': _L3_xattn_in['wk1'], 'L3_xattn_bk1': _L3_xattn_in['bk1'], 'L3_xattn_wv1': _L3_xattn_in['wv1'], 'L3_xattn_bv1': _L3_xattn_in['bv1'], 'L3_xattn_wo1': _L3_xattn_in['wo1'], 'L3_xattn_bo1': _L3_xattn_in['bo1'], 'L3_xattn_bias_k1': _L3_xattn_in['bias_k1'], 'L3_xattn_bias_v1': _L3_xattn_in['bias_v1'], 'L3_xattn_ln2_scale': _L3_xattn_in['ln2_scale'], 'L3_xattn_ln2_offset': _L3_xattn_in['ln2_offset'], 'L3_xattn_wq2': _L3_xattn_in['wq2'], 'L3_xattn_bq2': _L3_xattn_in['bq2'], 'L3_xattn_wk2': _L3_xattn_in['wk2'], 'L3_xattn_bk2': _L3_xattn_in['bk2'], 'L3_xattn_wv2': _L3_xattn_in['wv2'], 'L3_xattn_bv2': _L3_xattn_in['bv2'], 'L3_xattn_wo2': _L3_xattn_in['wo2'], 'L3_xattn_bo2': _L3_xattn_in['bo2'], 'L3_xattn_bias_k2': _L3_xattn_in['bias_k2'], 'L3_xattn_bias_v2': _L3_xattn_in['bias_v2'], 'L3_xattn_ln_mlp_scale': _L3_xattn_in['ln_mlp_scale'], 'L3_xattn_ln_mlp_offset': _L3_xattn_in['ln_mlp_offset'], 'L3_xattn_w_fc1': _L3_xattn_in['w_fc1'], 'L3_xattn_b_fc1': _L3_xattn_in['b_fc1'], 'L3_xattn_w_fc2': _L3_xattn_in['w_fc2'], 'L3_xattn_b_fc2': _L3_xattn_in['b_fc2']}

def reference(x, ctx_2048, mask_Bx1xSxS2_ff0, mask_1x1xSxS2_fc1, mask_Bx1xSxS2_ff1, L0_xattn_Wq, L0_xattn_bq, L0_xattn_Wk, L0_xattn_bk, L0_xattn_Wv, L0_xattn_bv, L0_xattn_Wo, L0_xattn_bo, L0_xattn_gamma, L0_xattn_beta, L1_xattn_ln1_s, L1_xattn_ln1_b, L1_xattn_w_qkv, L1_xattn_b_qkv, L1_xattn_w_ao, L1_xattn_b_ao, L1_xattn_ln2_s, L1_xattn_ln2_b, L1_xattn_w_q, L1_xattn_b_q, L1_xattn_w_kv, L1_xattn_b_kv, L1_xattn_w_co, L1_xattn_b_co, L1_xattn_ln3_s, L1_xattn_ln3_b, L1_xattn_w1, L1_xattn_b1, L1_xattn_w2, L1_xattn_b2, L2_xattn_ln1_scale, L2_xattn_ln1_offset, L2_xattn_wq1, L2_xattn_bq1, L2_xattn_wk1, L2_xattn_bk1, L2_xattn_wv1, L2_xattn_bv1, L2_xattn_wo1, L2_xattn_bo1, L2_xattn_bias_k1, L2_xattn_bias_v1, L2_xattn_ln2_scale, L2_xattn_ln2_offset, L2_xattn_wq2, L2_xattn_bq2, L2_xattn_wk2, L2_xattn_bk2, L2_xattn_wv2, L2_xattn_bv2, L2_xattn_wo2, L2_xattn_bo2, L2_xattn_bias_k2, L2_xattn_bias_v2, L2_xattn_ln_mlp_scale, L2_xattn_ln_mlp_offset, L2_xattn_w_fc1, L2_xattn_b_fc1, L2_xattn_w_fc2, L2_xattn_b_fc2, L3_xattn_ln1_scale, L3_xattn_ln1_offset, L3_xattn_wq1, L3_xattn_bq1, L3_xattn_wk1, L3_xattn_bk1, L3_xattn_wv1, L3_xattn_bv1, L3_xattn_wo1, L3_xattn_bo1, L3_xattn_bias_k1, L3_xattn_bias_v1, L3_xattn_ln2_scale, L3_xattn_ln2_offset, L3_xattn_wq2, L3_xattn_bq2, L3_xattn_wk2, L3_xattn_bk2, L3_xattn_wv2, L3_xattn_bv2, L3_xattn_wo2, L3_xattn_bo2, L3_xattn_bias_k2, L3_xattn_bias_v2, L3_xattn_ln_mlp_scale, L3_xattn_ln_mlp_offset, L3_xattn_w_fc1, L3_xattn_b_fc1, L3_xattn_w_fc2, L3_xattn_b_fc2):
    import jax
    import jax.numpy as jnp

    def _L0_xattn_ref(hidden_state, encoder_hidden_state, encoder_attention_mask, Wq, bq, Wk, bk, Wv, bv, Wo, bo, gamma, beta):
        import jax, jax.numpy as jnp
        import numpy as np
        H = 256
        NH = 32
        KVH = 8
        HD = H // NH
        GROUPS = NH // KVH
        EPS = 1e-06
        B, L, S = (4, 128, 128)

        def _gqa_forward(hidden_state, encoder_hidden_state, encoder_attention_mask, Wq, bq, Wk, bk, Wv, bv, Wo, bo, gamma, beta):
            b, l, _ = hidden_state.shape
            s = encoder_hidden_state.shape[1]
            q = hidden_state @ Wq + bq
            k = encoder_hidden_state @ Wk + bk
            v = encoder_hidden_state @ Wv + bv
            q = q.reshape(b, l, KVH, GROUPS, HD).transpose(0, 2, 3, 1, 4)
            k = k.reshape(b, s, KVH, HD).transpose(0, 2, 1, 3)
            v = v.reshape(b, s, KVH, HD).transpose(0, 2, 1, 3)
            scale = 1.0 / jnp.sqrt(jnp.asarray(HD, q.dtype))
            scores = jnp.einsum('bkgld,bksd->bkgls', q, k) * scale
            scores = scores + encoder_attention_mask[:, :, None, :, :]
            attn = jax.nn.softmax(scores, axis=-1)
            out = jnp.einsum('bkgls,bksd->bkgld', attn, v)
            out = out.transpose(0, 3, 1, 2, 4).reshape(b, l, H)
            out = out @ Wo + bo
            x = out + hidden_state
            mu = jnp.mean(x, axis=-1, keepdims=True)
            var = jnp.var(x, axis=-1, keepdims=True)
            return (x - mu) * jax.lax.rsqrt(var + EPS) * gamma + beta
        return _gqa_forward(hidden_state, encoder_hidden_state, encoder_attention_mask, Wq, bq, Wk, bk, Wv, bv, Wo, bo, gamma, beta)

    def _L1_xattn_ref(hidden_states, encoder_states, ltor_mask, cross_mask, ln1_s, ln1_b, w_qkv, b_qkv, w_ao, b_ao, ln2_s, ln2_b, w_q, b_q, w_kv, b_kv, w_co, b_co, ln3_s, ln3_b, w1, b1, w2, b2):
        import jax, jax.numpy as jnp
        import numpy as np
        H = 256
        NH = 16
        HD = H // NH
        EPS = 1e-05

        def gelu(x):
            return 0.5 * x * (1.0 + jnp.tanh(0.7978845608028654 * x * (1.0 + 0.044715 * x * x)))

        def layernorm(x, scale, bias):
            m = jnp.mean(x, axis=-1, keepdims=True)
            v = jnp.mean(jnp.square(x - m), axis=-1, keepdims=True)
            return (x - m) * jax.lax.rsqrt(v + EPS) * scale + bias

        def split_heads(x):
            b, s, _ = x.shape
            return x.reshape(b, s, NH, HD).transpose(0, 2, 1, 3)

        def merge_heads(x):
            b, nh, s, hd = x.shape
            return x.transpose(0, 2, 1, 3).reshape(b, s, nh * hd)

        def attention(q, k, v, mask):
            scores = jnp.einsum('bhqd,bhkd->bhqk', q, k) / jnp.sqrt(jnp.float32(HD))
            scores = scores * mask - 10000.0 * (1.0 - mask)
            probs = jax.nn.softmax(scores, axis=-1)
            return jnp.einsum('bhqk,bhkd->bhqd', probs, v)
        ln_out = layernorm(hidden_states, ln1_s, ln1_b)
        qkv = ln_out @ w_qkv + b_qkv
        q, k, v = jnp.split(qkv, 3, axis=-1)
        ctx = merge_heads(attention(split_heads(q), split_heads(k), split_heads(v), ltor_mask))
        attn_out = ctx @ w_ao + b_ao
        x = hidden_states + attn_out
        ln_out = layernorm(x, ln2_s, ln2_b)
        q = ln_out @ w_q + b_q
        kv = encoder_states @ w_kv + b_kv
        k, v = jnp.split(kv, 2, axis=-1)
        ctx = merge_heads(attention(split_heads(q), split_heads(k), split_heads(v), cross_mask))
        cross_out = ctx @ w_co + b_co
        x = x + cross_out
        ln_out = layernorm(x, ln3_s, ln3_b)
        mlp_out = gelu(ln_out @ w1 + b1) @ w2 + b2
        return x + mlp_out

    def _L2_xattn_ref(x, xf_1, xf_2, ln1_scale, ln1_offset, wq1, bq1, wk1, bk1, wv1, bv1, wo1, bo1, bias_k1, bias_v1, ln2_scale, ln2_offset, wq2, bq2, wk2, bk2, wv2, bv2, wo2, bo2, bias_k2, bias_v2, ln_mlp_scale, ln_mlp_offset, w_fc1, b_fc1, w_fc2, b_fc2):
        import jax, jax.numpy as jnp
        import numpy as np
        B, Q, S1, S2 = (4, 32, 256, 256)
        D, H, K, F = (256, 16, 128, 1024)
        LN_EPS = 1e-05

        def _layer_norm(x, scale, offset):
            mu = jnp.mean(x, axis=-1, keepdims=True)
            var = jnp.var(x, axis=-1, keepdims=True)
            return (x - mu) * jax.lax.rsqrt(var + LN_EPS) * scale + offset

        def _cross_attention(q_in, kv_in, wq, bq, wk, bk, wv, bv, wo, bo, bias_k, bias_v):
            b, q_len, _ = q_in.shape
            t = kv_in.shape[1]
            qh = (q_in @ wq + bq).reshape(b, q_len, H, K)
            kh = (kv_in @ wk + bk).reshape(b, t, H, K)
            vh = (kv_in @ wv + bv).reshape(b, t, H, K)
            kh = jnp.concatenate([kh, jnp.broadcast_to(bias_k, (b, 1, H, K))], axis=1)
            vh = jnp.concatenate([vh, jnp.broadcast_to(bias_v, (b, 1, H, K))], axis=1)
            scale = jnp.sqrt(jnp.asarray(K, q_in.dtype))
            logits = jnp.einsum('bqhk,bthk->bhqt', qh, kh) / scale
            weights = jax.nn.softmax(logits, axis=-1)
            ctx = jnp.einsum('bhqt,bthk->bqhk', weights, vh).reshape(b, q_len, H * K)
            return ctx @ wo + bo

        def _forward(x, xf_1, xf_2, ln1_scale, ln1_offset, wq1, bq1, wk1, bk1, wv1, bv1, wo1, bo1, bias_k1, bias_v1, ln2_scale, ln2_offset, wq2, bq2, wk2, bk2, wv2, bv2, wo2, bo2, bias_k2, bias_v2, ln_mlp_scale, ln_mlp_offset, w_fc1, b_fc1, w_fc2, b_fc2):
            res = x
            h = _layer_norm(x, ln1_scale, ln1_offset)
            x = res + _cross_attention(h, xf_1, wq1, bq1, wk1, bk1, wv1, bv1, wo1, bo1, bias_k1, bias_v1)
            res = x
            h = _layer_norm(x, ln2_scale, ln2_offset)
            x = res + _cross_attention(h, xf_2, wq2, bq2, wk2, bk2, wv2, bv2, wo2, bo2, bias_k2, bias_v2)
            h = _layer_norm(x, ln_mlp_scale, ln_mlp_offset)
            h = jax.nn.gelu(h @ w_fc1 + b_fc1, approximate=False) @ w_fc2 + b_fc2
            return x + h
        return _forward(x, xf_1, xf_2, ln1_scale, ln1_offset, wq1, bq1, wk1, bk1, wv1, bv1, wo1, bo1, bias_k1, bias_v1, ln2_scale, ln2_offset, wq2, bq2, wk2, bk2, wv2, bv2, wo2, bo2, bias_k2, bias_v2, ln_mlp_scale, ln_mlp_offset, w_fc1, b_fc1, w_fc2, b_fc2)

    def _L3_xattn_ref(x, xf_1, xf_2, ln1_scale, ln1_offset, wq1, bq1, wk1, bk1, wv1, bv1, wo1, bo1, bias_k1, bias_v1, ln2_scale, ln2_offset, wq2, bq2, wk2, bk2, wv2, bv2, wo2, bo2, bias_k2, bias_v2, ln_mlp_scale, ln_mlp_offset, w_fc1, b_fc1, w_fc2, b_fc2):
        import jax, jax.numpy as jnp
        import numpy as np
        B, Q, S1, S2 = (4, 32, 256, 256)
        D, H, K, F = (256, 16, 128, 1024)
        LN_EPS = 1e-05

        def _layer_norm(x, scale, offset):
            mu = jnp.mean(x, axis=-1, keepdims=True)
            var = jnp.var(x, axis=-1, keepdims=True)
            return (x - mu) * jax.lax.rsqrt(var + LN_EPS) * scale + offset

        def _cross_attention(q_in, kv_in, wq, bq, wk, bk, wv, bv, wo, bo, bias_k, bias_v):
            b, q_len, _ = q_in.shape
            t = kv_in.shape[1]
            qh = (q_in @ wq + bq).reshape(b, q_len, H, K)
            kh = (kv_in @ wk + bk).reshape(b, t, H, K)
            vh = (kv_in @ wv + bv).reshape(b, t, H, K)
            kh = jnp.concatenate([kh, jnp.broadcast_to(bias_k, (b, 1, H, K))], axis=1)
            vh = jnp.concatenate([vh, jnp.broadcast_to(bias_v, (b, 1, H, K))], axis=1)
            scale = jnp.sqrt(jnp.asarray(K, q_in.dtype))
            logits = jnp.einsum('bqhk,bthk->bhqt', qh, kh) / scale
            weights = jax.nn.softmax(logits, axis=-1)
            ctx = jnp.einsum('bhqt,bthk->bqhk', weights, vh).reshape(b, q_len, H * K)
            return ctx @ wo + bo

        def _forward(x, xf_1, xf_2, ln1_scale, ln1_offset, wq1, bq1, wk1, bk1, wv1, bv1, wo1, bo1, bias_k1, bias_v1, ln2_scale, ln2_offset, wq2, bq2, wk2, bk2, wv2, bv2, wo2, bo2, bias_k2, bias_v2, ln_mlp_scale, ln_mlp_offset, w_fc1, b_fc1, w_fc2, b_fc2):
            res = x
            h = _layer_norm(x, ln1_scale, ln1_offset)
            x = res + _cross_attention(h, xf_1, wq1, bq1, wk1, bk1, wv1, bv1, wo1, bo1, bias_k1, bias_v1)
            res = x
            h = _layer_norm(x, ln2_scale, ln2_offset)
            x = res + _cross_attention(h, xf_2, wq2, bq2, wk2, bk2, wv2, bv2, wo2, bo2, bias_k2, bias_v2)
            h = _layer_norm(x, ln_mlp_scale, ln_mlp_offset)
            h = jax.nn.gelu(h @ w_fc1 + b_fc1, approximate=False) @ w_fc2 + b_fc2
            return x + h
        return _forward(x, xf_1, xf_2, ln1_scale, ln1_offset, wq1, bq1, wk1, bk1, wv1, bv1, wo1, bo1, bias_k1, bias_v1, ln2_scale, ln2_offset, wq2, bq2, wk2, bk2, wv2, bv2, wo2, bo2, bias_k2, bias_v2, ln_mlp_scale, ln_mlp_offset, w_fc1, b_fc1, w_fc2, b_fc2)
    x = _L0_xattn_ref(x, ctx_2048, mask_Bx1xSxS2_ff0, L0_xattn_Wq, L0_xattn_bq, L0_xattn_Wk, L0_xattn_bk, L0_xattn_Wv, L0_xattn_bv, L0_xattn_Wo, L0_xattn_bo, L0_xattn_gamma, L0_xattn_beta)
    x = _L1_xattn_ref(x, ctx_2048, mask_1x1xSxS2_fc1, mask_Bx1xSxS2_ff1, L1_xattn_ln1_s, L1_xattn_ln1_b, L1_xattn_w_qkv, L1_xattn_b_qkv, L1_xattn_w_ao, L1_xattn_b_ao, L1_xattn_ln2_s, L1_xattn_ln2_b, L1_xattn_w_q, L1_xattn_b_q, L1_xattn_w_kv, L1_xattn_b_kv, L1_xattn_w_co, L1_xattn_b_co, L1_xattn_ln3_s, L1_xattn_ln3_b, L1_xattn_w1, L1_xattn_b1, L1_xattn_w2, L1_xattn_b2)
    x = _L2_xattn_ref(x, ctx_2048, ctx_2048, L2_xattn_ln1_scale, L2_xattn_ln1_offset, L2_xattn_wq1, L2_xattn_bq1, L2_xattn_wk1, L2_xattn_bk1, L2_xattn_wv1, L2_xattn_bv1, L2_xattn_wo1, L2_xattn_bo1, L2_xattn_bias_k1, L2_xattn_bias_v1, L2_xattn_ln2_scale, L2_xattn_ln2_offset, L2_xattn_wq2, L2_xattn_bq2, L2_xattn_wk2, L2_xattn_bk2, L2_xattn_wv2, L2_xattn_bv2, L2_xattn_wo2, L2_xattn_bo2, L2_xattn_bias_k2, L2_xattn_bias_v2, L2_xattn_ln_mlp_scale, L2_xattn_ln_mlp_offset, L2_xattn_w_fc1, L2_xattn_b_fc1, L2_xattn_w_fc2, L2_xattn_b_fc2)
    x = _L3_xattn_ref(x, ctx_2048, ctx_2048, L3_xattn_ln1_scale, L3_xattn_ln1_offset, L3_xattn_wq1, L3_xattn_bq1, L3_xattn_wk1, L3_xattn_bk1, L3_xattn_wv1, L3_xattn_bv1, L3_xattn_wo1, L3_xattn_bo1, L3_xattn_bias_k1, L3_xattn_bias_v1, L3_xattn_ln2_scale, L3_xattn_ln2_offset, L3_xattn_wq2, L3_xattn_bq2, L3_xattn_wk2, L3_xattn_bk2, L3_xattn_wv2, L3_xattn_bv2, L3_xattn_wo2, L3_xattn_bo2, L3_xattn_bias_k2, L3_xattn_bias_v2, L3_xattn_ln_mlp_scale, L3_xattn_ln_mlp_offset, L3_xattn_w_fc1, L3_xattn_b_fc1, L3_xattn_w_fc2, L3_xattn_b_fc2)
    return x

_drawn_inputs = setup_inputs


def setup_inputs(seed=0):
    import zlib

    import numpy as np

    out = dict(_drawn_inputs(seed))
    spreads = {'L0_xattn_bq': (0.0, 0.8),
     'L0_xattn_bk': (0.0, 2.0),
     'L0_xattn_bv': (0.0, 0.1),
     'L0_xattn_bo': (0.0, 0.1),
     'L0_xattn_gamma': (1.0, 0.2),
     'L0_xattn_beta': (0.0, 0.1),
     'L1_xattn_ln1_s': (1.0, 0.6),
     'L1_xattn_ln1_b': (0.0, 0.8),
     'L1_xattn_b_qkv': (0.0, 0.302),
     'L1_xattn_b_ao': (0.0, 0.1),
     'L1_xattn_ln2_s': (1.0, 0.6),
     'L1_xattn_ln2_b': (0.0, 2.0),
     'L1_xattn_b_q': (0.0, 2.0),
     'L1_xattn_b_kv': (0.0, 0.294),
     'L1_xattn_b_co': (0.0, 0.1),
     'L1_xattn_ln3_s': (1.0, 0.6),
     'L1_xattn_ln3_b': (0.0, 0.8),
     'L1_xattn_b1': (0.0, 0.1),
     'L1_xattn_b2': (0.0, 0.1),
     'L2_xattn_ln1_scale': (1.0, 0.6),
     'L2_xattn_ln1_offset': (0.0, 0.8),
     'L2_xattn_bq1': (0.0, 0.8),
     'L2_xattn_bk1': (0.0, 2.0),
     'L2_xattn_bv1': (0.0, 0.1),
     'L2_xattn_bo1': (0.0, 0.1),
     'L2_xattn_ln2_scale': (1.0, 0.6),
     'L2_xattn_ln2_offset': (0.0, 0.8),
     'L2_xattn_bq2': (0.0, 0.8),
     'L2_xattn_bk2': (0.0, 2.0),
     'L2_xattn_bv2': (0.0, 0.1),
     'L2_xattn_bo2': (0.0, 0.1),
     'L2_xattn_ln_mlp_scale': (1.0, 0.6),
     'L2_xattn_ln_mlp_offset': (0.0, 0.8),
     'L2_xattn_b_fc1': (0.0, 0.1),
     'L2_xattn_b_fc2': (0.0, 0.1),
     'L3_xattn_ln1_scale': (1.0, 0.6),
     'L3_xattn_ln1_offset': (0.0, 0.8),
     'L3_xattn_bq1': (0.0, 0.8),
     'L3_xattn_bk1': (0.0, 2.0),
     'L3_xattn_bv1': (0.0, 0.1),
     'L3_xattn_bo1': (0.0, 0.1),
     'L3_xattn_ln2_scale': (1.0, 0.6),
     'L3_xattn_ln2_offset': (0.0, 0.8),
     'L3_xattn_bq2': (0.0, 0.8),
     'L3_xattn_bk2': (0.0, 2.0),
     'L3_xattn_bv2': (0.0, 0.1),
     'L3_xattn_bo2': (0.0, 0.1),
     'L3_xattn_ln_mlp_scale': (1.0, 0.6),
     'L3_xattn_ln_mlp_offset': (0.0, 0.8),
     'L3_xattn_b_fc1': (0.0, 0.279),
     'L3_xattn_b_fc2': (0.0, 0.1)}
    factors = {'L0_xattn_Wq': 8.0,
     'L0_xattn_Wk': 8.0,
     'L1_xattn_w_qkv': 3.323,
     'L1_xattn_w_q': 8.0,
     'L2_xattn_wq1': 8.0,
     'L2_xattn_wk1': 8.0,
     'L2_xattn_bias_k1': 64.0,
     'L2_xattn_bias_v1': 64.0,
     'L2_xattn_wq2': 8.0,
     'L2_xattn_wk2': 8.0,
     'L2_xattn_bias_k2': 64.0,
     'L2_xattn_bias_v2': 64.0,
     'L3_xattn_wq1': 8.0,
     'L3_xattn_wk1': 8.0,
     'L3_xattn_bias_k1': 64.0,
     'L3_xattn_bias_v1': 64.0,
     'L3_xattn_wq2': 8.0,
     'L3_xattn_wk2': 8.0,
     'L3_xattn_bias_k2': 64.0,
     'L3_xattn_bias_v2': 64.0}
    for name, (base, spread) in spreads.items():
        noise = np.random.default_rng([zlib.crc32(name.encode()), seed]).standard_normal(out[name].shape)
        drawn = base * np.exp(spread * noise) if base else spread * noise
        out[name] = jnp.asarray(drawn.astype(out[name].dtype))
    for name, factor in factors.items():
        out[name] = (out[name] * factor).astype(out[name].dtype)
    return out
```

```python
from contextlib import ExitStack
from math import sqrt

import concourse.bass as bass
from concourse import mybir

F32 = mybir.dt.float32
F32R = mybir.dt.float32r
ALU = mybir.AluOpType
ACT = mybir.ActivationFunctionType
AX = mybir.AxisListType

P = 128
B, S, D = 4, 256, 256
N = B * S
RT = N // P
DT = D // P
BANK = 512
HALF = N // BANK

QKV_DUP = 256
BH, BK = 16, 128
PAIRS = BH // 2
KC = S + 2
F = 1024
FT = F // P


def hi_passes(a_hi, a_lo, b_hi, b_lo):
    return ((a_hi, b_hi), (a_hi, b_lo), (a_lo, b_hi))


class VecLayout:

    def __init__(self):
        self.n = 0
        self.at = {}

    def add(self, name, width):
        self.at[name] = self.n
        self.n += width


VEC = VecLayout()
for _a in range(3):
    for _v in ("bq", "bk", "bv"):
        VEC.add(f"s{_a}_{_v}", 2)
for _v in ("ln1", "ln2", "ln3"):
    VEC.add(f"L1_{_v}_s", 2)
    VEC.add(f"L1_{_v}_b", 2)
VEC.add("L1_b1", FT)
HEADV = 3
ATT_W = BH * HEADV + 4 + 2 * BH
VEC.add("att", 4 * ATT_W)
MLP_W = 4 + FT
VEC.add("mlp", 2 * MLP_W)


def program(nc, io):
    out = io["out"]
    top = ExitStack()

    def sbt(ctx, name, shape, dt=F32):
        return ctx.enter_context(nc.sbuf_tensor(name, shape, dt))

    def sem(name):
        return top.enter_context(nc.semaphore(name))

    PS = top.enter_context(nc.psum_tensor("PS", [P, 8, BANK], F32))
    X = sbt(top, "X", [P, RT, D])
    ctx_hi = sbt(top, "ctx_hi", [P, DT, N], F32R)
    ctx_lo = sbt(top, "ctx_lo", [P, DT, N], F32R)
    h_hi = sbt(top, "h_hi", [P, DT, N], F32R)
    h_lo = sbt(top, "h_lo", [P, DT, N], F32R)
    vec = sbt(top, "vec", [P, VEC.n])
    ident = sbt(top, "ident", [P, P])
    stats = sbt(top, "stats", [P, RT, 6])
    moments = sbt(top, "moments", [P, RT, 2])
    rstd = sbt(top, "rstd", [P, RT])
    vareps = sbt(top, "vareps", [P, RT])
    newt = sbt(top, "newt", [P, RT])
    hf = sbt(top, "hf", [P, 2, BANK])

    const_ld = sem("const_ld")
    x_ld = sem("x_ld")
    c_ld = sem("c_ld")
    ring_full = sem("ring_full")
    ring_hi = sem("ring_hi")
    ring_free = sem("ring_free")
    w_ld = sem("w_ld")
    w_scaled = sem("w_scaled")
    w_hi = sem("w_hi")
    w_lo = sem("w_lo")
    ln_step = sem("ln_step")
    ln_sqrt = sem("ln_sqrt")
    xn_ready = sem("xn_ready")
    hf_full = sem("hf_full")
    hf_hi = sem("hf_hi")
    h_ready = sem("h_ready")
    st_done = sem("st_done")
    bias_ready = sem("bias_ready")

    count = {}

    def now(name):
        return count.get(name, 0)

    def vcol(name, i=0):
        c = VEC.at[name] + i
        return vec[:, c:c + 1]

    LN_STEPS = 2 * RT + 6

    def tile_stats(tiles):
        for rt in tiles:
            nc.vector.bn_stats(stats[:, rt, :], X[:, rt, :]).then_inc(ln_step, 1)

    def ln_stats(v, base, eps, sqrt_n):
        k = RT
        v.wait_ge(ln_step, base + RT)
        nc.vector.memset(newt[:, 0:1], 0.0)
        for rt in range(RT):
            nc.vector.bn_aggr(moments[:, rt, :], stats[:, rt, :]).then_inc(ln_step, 1)
        k += RT
        v.wait_ge(ln_step, base + k)
        nc.vector.tensor_scalar(vareps[:], moments[:, :, 1], eps, None, ALU.add).then_inc(ln_step, 1)
        k += 1
        v.wait_ge(ln_sqrt, sqrt_n)
        nc.vector.reciprocal(rstd[:], rstd[:]).then_inc(ln_step, 1)
        k += 1
        v.wait_ge(ln_step, base + k)
        nc.vector.tensor_tensor(newt[:], rstd[:], rstd[:], ALU.mult).then_inc(ln_step, 1)
        k += 1
        v.wait_ge(ln_step, base + k)
        nc.vector.tensor_tensor(newt[:], newt[:], vareps[:], ALU.mult).then_inc(ln_step, 1)
        k += 1
        v.wait_ge(ln_step, base + k)
        nc.vector.tensor_scalar(newt[:], newt[:], -0.5, 1.5, ALU.mult, ALU.add).then_inc(ln_step, 1)
        k += 1
        v.wait_ge(ln_step, base + k)
        nc.vector.tensor_tensor(rstd[:], rstd[:], newt[:], ALU.mult).then_inc(ln_step, 1)
        k += 1
        assert k == LN_STEPS
        v.wait_ge(ln_step, base + k)

    def ln_root(a, base):
        a.wait_ge(ln_step, base + 2 * RT + 1)
        nc.scalar.activation(rstd[:], vareps[:], ACT.Sqrt).then_inc(ln_sqrt, 1)

    def ln_normalise(v, dst):
        for rt in range(RT):
            nc.vector.tensor_scalar(dst[:, rt, :], X[:, rt, :], moments[:, rt, 0:1], rstd[:, rt:rt + 1],
                                    ALU.subtract, ALU.mult).then_inc(xn_ready, 1)

    TURNS = [(h, dt) for h in range(HALF) for dt in range(DT)]

    def turn_pe(t, src, bank_of, base_ring, first, xn_base):
        for j, (h, dt) in enumerate(TURNS):
            n = first + j
            if xn_base is not None:
                t.wait_ge(xn_ready, xn_base + 4 * h + 4)
            ring_take(t, base_ring, n, len(bank_of))
            ps = PS[:, bank_of[n % len(bank_of)], :]
            for r in range(4):
                mm = nc.tensor.transpose(ps[:, r * P:(r + 1) * P], src[:, 4 * h + r, dt * P:(dt + 1) * P], ident[:])
            mm.then_inc(ring_full, 1)

    def ring_take(t, base_ring, n, banks):
        if n >= banks:
            t.wait_ge(ring_free, base_ring + n - banks + 1)

    def affine_dve(v, bank_of, base_ring, first, base_hf, scale_of, shift_of):
        for j in range(len(TURNS) + 1):
            if j < len(TURNS):
                n = first + j
                h, dt = TURNS[j]
                v.wait_ge(ring_full, base_ring + n + 1)
                if j >= 2:
                    v.wait_ge(h_ready, base_hf + j - 1)
                nc.vector.tensor_scalar(hf[:, j % 2, :], PS[:, bank_of[n % len(bank_of)], :],
                                        scale_of(dt), shift_of(dt), ALU.mult, ALU.add).then_inc(ring_free, 1)
            if j >= 1:
                h, dt = TURNS[j - 1]
                v.wait_ge(hf_hi, base_hf + j)
                nc.vector.tensor_tensor(h_lo[:, dt, h * BANK:(h + 1) * BANK], hf[:, (j - 1) % 2, :],
                                        h_hi[:, dt, h * BANK:(h + 1) * BANK].bitcast(F32),
                                        ALU.subtract).then_inc(h_ready, 1)

    def affine_act(a, base_ring, first, base_hf):
        for j, (h, dt) in enumerate(TURNS):
            a.wait_ge(ring_free, base_ring + first + j + 1)
            nc.scalar.activation(h_hi[:, dt, h * BANK:(h + 1) * BANK], hf[:, j % 2, :], ACT.Copy).then_inc(hf_hi, 1)

    small = ExitStack()
    xn = sbt(small, "xn", [P, RT, D])
    q_hi = sbt(small, "q_hi", [P, 2, N], F32R)
    q_lo = sbt(small, "q_lo", [P, 2, N], F32R)
    k_hi = sbt(small, "k_hi", [P, 2, N], F32R)
    k_lo = sbt(small, "k_lo", [P, 2, N], F32R)

    wo_hi = sbt(small, "wo_hi", [P, DT, D], F32R)
    wo_lo = sbt(small, "wo_lo", [P, DT, D], F32R)
    bo_row = sbt(small, "bo_row", [P, D])
    gb_rows = sbt(small, "gb_rows", [P, 2, D])
    sel = sbt(small, "sel", [16, 2, P])
    v_rows = xn
    scope_proj = ExitStack()
    wst = sbt(scope_proj, "wst", [P, 4, DT, D])
    wq_hi = sbt(scope_proj, "wq_hi", [P, DT, D], F32R)
    wq_lo = sbt(scope_proj, "wq_lo", [P, DT, D], F32R)
    wk_hi = sbt(scope_proj, "wk_hi", [P, DT, D], F32R)
    wk_lo = sbt(scope_proj, "wk_lo", [P, DT, D], F32R)
    wv_hi = sbt(scope_proj, "wv_hi", [P, DT, D], F32R)
    wv_lo = sbt(scope_proj, "wv_lo", [P, DT, D], F32R)
    scope_proj.close()
    scope_att = ExitStack()
    smul = sbt(scope_att, "smul", [P, 2, BANK])
    sm = sbt(scope_att, "sm", [P, 3, BANK])
    pr = sbt(scope_att, "pr", [P, 4, BANK])
    pt = sbt(scope_att, "pt", [P, 3, BANK])
    q_st = sbt(scope_att, "q_st", [P, 4, N], F32R)
    k_st = sbt(scope_att, "k_st", [P, 4, N], F32R)
    v_win = sbt(scope_att, "v_win", [P, RT, 1136])
    mask = sbt(scope_att, "mask", [P, B, 2, S])
    mask_add = sbt(scope_att, "mask_add", [P, B, 2, S])
    nmax = sbt(scope_att, "nmax", [P, 4, 2])
    pace = sbt(scope_att, "pace", [P, 8])
    sums = sbt(scope_att, "sums", [P, B, 2, 16])
    rsum = sbt(scope_att, "rsum", [P, B, 2, 16])
    rt_sb = sbt(scope_att, "rt_sb", [16, 2, S])
    rx_sb = hf[:, 0, :].rearrange("p (a n) -> p a n", a=2)
    of_sb = hf[:, 1, :].rearrange("p (a n) -> p a n", a=2)
    scope_att.close()
    scope_mw = ExitStack()
    mws1 = sbt(scope_mw, "mws1", [P, DT, F])
    mws2 = sbt(scope_mw, "mws2", [P, FT, D])
    mw1h = sbt(scope_mw, "mw1h", [P, DT, F], F32R)
    mw1l = sbt(scope_mw, "mw1l", [P, DT, F], F32R)
    mw2h = sbt(scope_mw, "mw2h", [P, FT, D], F32R)
    mw2l = sbt(scope_mw, "mw2l", [P, FT, D], F32R)
    b2s_row = sbt(scope_mw, "b2s_row", [P, D])
    gs_hi = sbt(scope_mw, "gs_hi", [P, FT, N], F32R)
    gs_lo = sbt(scope_mw, "gs_lo", [P, FT, N], F32R)
    scope_mw.close()
    m_ld = sem("m_ld")
    w_kind = [sem(f"w_ld{i}") for i in range(4)]
    stack_ld = [sem(f"stack_ld{g}") for g in range(4)]
    win_zero = sem("win_zero")
    win_ready = sem("win_ready")
    xb_ready = sem("xb_ready")
    ma_ready = sem("ma_ready")
    score_done = sem("score_done")
    mul_done = sem("mul_done")
    max_done = sem("max_done")
    exp_done = sem("exp_done")
    turn_done = sem("turn_done")
    pt_v = sem("pt_v")
    pt_a = sem("pt_a")
    pv_done = sem("pv_done")
    rs_done = sem("rs_done")
    rt_done = sem("rt_done")
    rt_copied = sem("rt_copied")
    rx_done = sem("rx_done")
    rx_copied = sem("rx_copied")
    o_mul = sem("o_mul")
    o_hi = sem("o_hi")
    o_ready = sem("o_ready")

    def weights_load(sp, idx):
        hd8 = idx == 0
        for i, kind in enumerate("qkvo"):
            w = io[f"sw{kind}"][idx] if not (hd8 and kind == "v") else io["swv0"]
            dst = wst[:, i, :, 0:64] if hd8 and kind == "v" else wst[:, i]
            sp.dma_start(dst, w.rearrange("(t p) n -> p t n", p=P)).then_inc(w_kind[i], 16)

    def weights_act(a, idx):
        a.wait_ge(w_kind[0], now("w_kind") + 16)
        nc.scalar.activation(wst[:, 0], wst[:, 0], ACT.Copy, scale=1.0 / sqrt(8 if idx == 0 else 16)).then_inc(w_scaled, 1)
        for i, dst in enumerate((wq_hi, wk_hi, wv_hi, wo_hi)):
            w = 64 if idx == 0 and i == 2 else D
            if i == 0:
                a.wait_ge(w_scaled, now("w_scaled") + 1)
            else:
                a.wait_ge(w_kind[i], now("w_kind") + 16)
            nc.scalar.activation(dst[:, :, 0:w], wst[:, i, :, 0:w], ACT.Copy).then_inc(w_hi, 1)

    def weights_pool(p, idx):
        for i, (hi, lo) in enumerate(((wq_hi, wq_lo), (wk_hi, wk_lo), (wv_hi, wv_lo), (wo_hi, wo_lo))):
            w = 64 if idx == 0 and i == 2 else D
            p.wait_ge(w_hi, now("w_hi") + i + 1)
            nc.gpsimd.tensor_tensor(lo[:, :, 0:w], wst[:, i, :, 0:w], hi[:, :, 0:w].bitcast(F32),
                                    ALU.subtract).then_inc(w_lo, 1)

    def weights_count():
        for nm, k in (("w_kind", 16), ("w_scaled", 1), ("w_hi", 4), ("w_lo", 4)):
            count[nm] = count.get(nm, 0) + k

    all_banks = list(range(8))
    with nc.Block() as block:

        @block.sync
        def _(sp):
            sp.dma_start(ident[:], io["ident"]).then_inc(const_ld, 16)
            sp.dma_start(xn[:], io["ctx"].rearrange("(r p) d -> p r d", p=P)).then_inc(c_ld, 16)
            sp.dma_start(X[:], io["x"].rearrange("(r p) d -> p r d", p=P)).then_inc(x_ld, 16)
            sp.dma_start(vec[:], io["vec"]).then_inc(const_ld, 16)
            weights_load(sp, 0)

        @block.gpsimd
        def _(p):
            weights_pool(p, 0)

        @block.tensor
        def _(t):
            t.wait_ge(const_ld, 32)
            t.wait_ge(c_ld, 16)
            turn_pe(t, xn, all_banks, 0, 0, None)
            t.wait_ge(x_ld, 16)
            turn_pe(t, X, all_banks, 0, len(TURNS), None)

        @block.scalar
        def _(a):
            for n in range(2 * len(TURNS)):
                h, dt = TURNS[n % len(TURNS)]
                dst = ctx_hi if n < len(TURNS) else h_hi
                a.wait_ge(ring_full, n + 1)
                nc.scalar.activation(dst[:, dt, h * BANK:(h + 1) * BANK], PS[:, n, :], ACT.Copy).then_inc(ring_hi, 1)
            weights_act(a, 0)

        @block.vector
        def _(v):
            for n in range(2 * len(TURNS)):
                h, dt = TURNS[n % len(TURNS)]
                hi, lo = (ctx_hi, ctx_lo) if n < len(TURNS) else (h_hi, h_lo)
                v.wait_ge(ring_hi, n + 1)
                nc.vector.tensor_tensor(lo[:, dt, h * BANK:(h + 1) * BANK], PS[:, n, :],
                                        hi[:, dt, h * BANK:(h + 1) * BANK].bitcast(F32),
                                        ALU.subtract).then_inc(ring_free, 1)
            v.wait_ge(const_ld, 32)
            s = 1.0 / sqrt(BK)
            for at in range(4):
                c = VEC.at["att"] + at * ATT_W
                bq = vec[:, c:c + BH * HEADV].rearrange("p (h v) -> p h v", v=HEADV)[:, :, 0]
                nc.vector.tensor_scalar(bq, bq, s, None, ALU.mult).then_inc(bias_ready, 1)
                ln = vec[:, c + BH * HEADV:c + BH * HEADV + 4]
                nc.vector.tensor_scalar(ln, ln, s, None, ALU.mult).then_inc(bias_ready, 1)
            for a3 in (0, 1, 2):
                hd = 8 if a3 == 0 else 16
                c = VEC.at[f"s{a3}_bq"]
                nc.vector.tensor_scalar(vec[:, c:c + 2], vec[:, c:c + 2], 1.0 / sqrt(hd), None,
                                        ALU.mult).then_inc(bias_ready, 1)

    count.update(ring_full=8, ring_hi=8, ring_free=8, bias_ready=11)
    weights_count()

    def small_attention(idx, HD, additive, src_hi, src_lo, mask_io, per_batch):
        base = dict(count)

        def b0(name):
            return base.get(name, 0)

        heads_t = P // HD
        G = 32 // HD
        KROWS = 4 * HD
        NV = (4 if HD == 8 else heads_t)
        VW = D if HD == 16 else 64
        PAD = P - HD
        U = 4 * B * G
        unit = [(g, b, j) for g in range(4) for b in range(B) for j in range(G)]
        last = [3 * B * G + b * G + G - 1 for b in range(B)]
        LX = 1 if additive else 2
        LT, LC, LV = LX + 1, LX + 2, LX + 3
        STEPS = U + LV + 2
        RB = 4
        jobs = [("q", m, h) for m in range(2) for h in range(HALF)] + \
               [("k", m, h) for m in range(2) for h in range(HALF)] + [("v", i, 0) for i in range(4)]
        V0 = sum(1 for j in jobs if j[0] != "v")

        def evac_on_v(i):
            return additive and i % 2 == 0

        def n_v(i):
            return (i // 2 + 1) if additive else 0

        def n_a(i):
            return ((i + 1) // 2) if additive else i + 1

        NV_M = U // 2 if additive else 0
        NA_M = U // 2 if additive else U

        with nc.Block() as block:

            @block.sync
            def _(sp):
                if per_batch:
                    for b in range(B):
                        sp.dma_start(mask[:, b], mask_io[b].rearrange("(r p) n -> p r n", p=P)).then_inc(m_ld, 16)
                else:
                    sp.dma_start(mask[:, 0], mask_io.rearrange("(r p) n -> p r n", p=P)).then_inc(m_ld, 16)
                sp.dma_start(bo_row[:], io["sbo"][idx:idx + 1, :].to_broadcast([P, D])).then_inc(m_ld, 16)
                if idx == 0:
                    sp.dma_start(sel[:], io["sel"]).then_inc(m_ld, 16)
                for m in range(2):
                    for g in range(4):
                        if m == 1:
                            sp.wait_ge(score_done, b0("score_done") + (g + 1) * B * G)
                        for w, (hi, lo, st) in enumerate(((q_hi, q_lo, q_st), (k_hi, k_lo, k_st))):
                            if g == 0:
                                sp.wait_ge(ring_free, b0("ring_free") + 4 * w + 2 * m + 2)
                            for part in range(4):
                                srct = (hi, hi, lo, lo)[part] if w == 0 else (hi, lo, hi, lo)[part]
                                sp.dma_start(st[part:P:4, g, :].bitcast(F32),
                                             srct[32 * g:32 * g + 32, m, :].bitcast(F32)).then_inc(stack_ld[g], 16)
                for g in range(4):
                    sp.wait_ge(stack_ld[g], b0("stack_ld") + 256)

            @block.gpsimd
            def _(p):
                nc.gpsimd.memset(v_win[:], 0.0).then_inc(win_zero, 1)
                n_m = 16 * ((B if per_batch else 1) + 1 + (idx == 0))
                p.wait_ge(m_ld, b0("m_ld") + n_m)
                if not additive:
                    nb = B if per_batch else 1
                    nc.gpsimd.tensor_scalar(mask_add[:, 0:nb], mask[:, 0:nb], 1.0, 10000.0,
                                            ALU.subtract, ALU.mult).then_inc(ma_ready, 1)
                nc.gpsimd.tensor_tensor(X[:], X[:], bo_row[:].unsqueeze(1).to_broadcast([P, RT, D]),
                                        ALU.add).then_inc(xb_ready, 1)

            @block.tensor
            def _(t):
                for n, (kind, i, h) in enumerate(jobs):
                    ring_take(t, b0("ring_free"), n, RB)
                    ps = PS[:, n % RB, :]
                    if kind == "v":
                        for r in range(2):
                            tt = 2 * i + r
                            k = 0
                            for dt in range(DT):
                                c = slice(tt * P, (tt + 1) * P)
                                for lhs, rhs in hi_passes(src_hi[:, dt, c], src_lo[:, dt, c],
                                                          wv_hi[:, dt, 0:VW], wv_lo[:, dt, 0:VW]):
                                    mm = nc.tensor.matmul(ps[:, r * VW:(r + 1) * VW], lhs, rhs,
                                                          start=(k == 0), stop=(k == 5))
                                    k += 1
                    else:
                        wh, wl = (wq_hi, wq_lo) if kind == "q" else (wk_hi, wk_lo)
                        xh, xl = (h_hi, h_lo) if kind == "q" else (src_hi, src_lo)
                        k = 0
                        for dt in range(DT):
                            c = slice(h * BANK, (h + 1) * BANK)
                            w = slice(i * P, (i + 1) * P)
                            for lhs, rhs in hi_passes(wh[:, dt, w], wl[:, dt, w], xh[:, dt, c], xl[:, dt, c]):
                                mm = nc.tensor.matmul(ps[:], lhs, rhs, start=(k == 0), stop=(k == 5))
                                k += 1
                    mm.then_inc(ring_full, 1)
                t.wait_ge(ring_free, b0("ring_free") + len(jobs))
                with t.Fori(0, 2) as m:
                    for s in range(STEPS):
                        if s < U:
                            g, b, j = unit[s]
                            if b == 0 and j == 0:
                                t.wait_ge(stack_ld[g], m * 128 + (b0("stack_ld") + 128))
                            if s >= 2:
                                t.wait_ge(max_done if additive else mul_done,
                                          m * U + (b0("max_done" if additive else "mul_done") + s - 1))
                            rows = slice(KROWS * j, KROWS * (j + 1))
                            for qt in range(2):
                                c = b * S + qt * P
                                mm = nc.tensor.matmul(PS[:, s % 2, qt * S:(qt + 1) * S], q_st[rows, g, c:c + P],
                                                      k_st[rows, g, b * S:(b + 1) * S], start=True, stop=True)
                            mm.then_inc(score_done, 1)
                        i = s - LT
                        if 0 <= i < U:
                            t.wait_ge(exp_done, m * U + (b0("exp_done") + i + 1))
                            if i >= 2:
                                if evac_on_v(i - 2):
                                    t.wait_ge(pt_v, m * NV_M + (b0("pt_v") + n_v(i - 2)))
                                else:
                                    t.wait_ge(pt_a, m * NA_M + (b0("pt_a") + n_a(i - 2)))
                            for tt in range(2):
                                for qt in range(2):
                                    mm = nc.tensor.transpose(
                                        PS[:, 2 + i % 2, tt * S + qt * P:tt * S + (qt + 1) * P],
                                        pr[:, i % 4, qt * S + tt * P:qt * S + (tt + 1) * P], ident[:])
                            mm.then_inc(turn_done, 1)
                        i = s - LV
                        if 0 <= i < U:
                            g, b, j = unit[i]
                            if i == 0:
                                t.wait_ge(win_ready, m + (b0("win_ready") + 1))
                            if evac_on_v(i):
                                t.wait_ge(pt_v, m * NV_M + (b0("pt_v") + n_v(i)))
                            else:
                                t.wait_ge(pt_a, m * NA_M + (b0("pt_a") + n_a(i)))
                            pos = g * G + j
                            kv = g if HD == 8 else pos
                            w0 = PAD + P * kv - HD * pos
                            for tt in range(2):
                                mm = nc.tensor.matmul(PS[:, 4 + b, 0:S], v_win[:, 2 * b + tt, w0:w0 + P],
                                                      pt[:, i % 3, tt * S:(tt + 1) * S],
                                                      start=(pos == 0 and tt == 0),
                                                      stop=(pos == heads_t - 1 and tt == 1))
                            mm.then_inc(pv_done, 1)
                        for b in range(B):
                            if s == last[b] + LV:
                                t.wait_ge(rs_done, m * B + (b0("rs_done") + b + 1))
                                for qt in range(2):
                                    mm = nc.tensor.transpose(PS[0:heads_t, 4 + b, S + qt * P:S + (qt + 1) * P],
                                                             rsum[:, b, qt, 0:heads_t], ident[:])
                                mm.then_inc(rt_done, 1)
                            if s == last[b] + LV + 1:
                                t.wait_ge(rt_copied, m * B + (b0("rt_copied") + b + 1))
                                nc.tensor.matmul(PS[:, 4 + b, S:2 * S], sel[0:heads_t, 0 if HD == 8 else 1, :],
                                                 rt_sb[0:heads_t, b % 2, :], start=True,
                                                 stop=True).then_inc(rx_done, 1)
                for n in range(4):
                    t.wait_ge(o_ready, b0("o_ready") + 2 * B)
                    for r in range(2):
                        c = slice((2 * n + r) * P, (2 * n + r + 1) * P)
                        k = 0
                        for m2 in range(2):
                            for lhs, rhs in hi_passes(q_hi[:, m2, c], q_lo[:, m2, c], wo_hi[:, m2, :], wo_lo[:, m2, :]):
                                mm = nc.tensor.matmul(PS[:, n, r * D:(r + 1) * D], lhs, rhs,
                                                      start=(k == 0), stop=(k == 5))
                                k += 1
                    mm.then_inc(ring_full, 1)

            @block.scalar
            def _(a):
                for n, (kind, i, h) in enumerate(jobs):
                    if kind == "v":
                        continue
                    a.wait_ge(ring_full, b0("ring_full") + n + 1)
                    dst = q_hi if kind == "q" else k_hi
                    nc.scalar.activation(dst[:, i, h * BANK:(h + 1) * BANK], PS[:, n % RB, :], ACT.Identity,
                                         bias=vcol(f"s{idx}_b{kind}", i)).then_inc(ring_hi, 1)
                with a.Fori(0, 2) as m:
                    for s in range(STEPS):
                        i = s - LC
                        if 0 <= i < U and not evac_on_v(i):
                            a.wait_ge(turn_done, m * U + (b0("turn_done") + i + 1))
                            if i >= 3:
                                a.wait_ge(pv_done, m * U + (b0("pv_done") + i - 2))
                            nc.scalar.activation(pt[:, i % 3, :], PS[:, 2 + i % 2, :], ACT.Copy).then_inc(pt_a, 1)
                        i = s - LX
                        if 0 <= i < U:
                            g, b, j = unit[i]
                            a.wait_ge(max_done, m * U + (b0("max_done") + i + 1))
                            if i >= 4:
                                a.wait_ge(turn_done, m * U + (b0("turn_done") + i - 3))
                            for qt in range(2):
                                e = nc.scalar.activation(pr[:, i % 4, qt * S:(qt + 1) * S],
                                                         sm[:, i % 3, qt * S:(qt + 1) * S], ACT.Exp,
                                                         bias=nmax[:, i % 4, qt:qt + 1], scale=-1.0,
                                                         accum_out=sums[:, b, qt, g * G + j:g * G + j + 1])
                            e.then_inc(exp_done, 1)
                        for b in range(B):
                            if s == last[b] + LV:
                                a.wait_ge(rt_done, m * B + (b0("rt_done") + b + 1))
                                nc.scalar.activation(rt_sb[0:heads_t, b % 2, :], PS[0:heads_t, 4 + b, S:2 * S],
                                                     ACT.Copy).then_inc(rt_copied, 1)
                            if s == last[b] + LV + 1:
                                a.wait_ge(rx_done, m * B + (b0("rx_done") + b + 1))
                                if b >= 2:
                                    a.wait_ge(o_mul, m * B + (b0("o_mul") + b - 1))
                                nc.scalar.activation(rx_sb[:, b % 2, :], PS[:, 4 + b, S:2 * S],
                                                     ACT.Copy).then_inc(rx_copied, 1)

            @block.vector
            def _(v):
                for n, (kind, i, h) in enumerate(jobs):
                    ps = PS[:, n % RB, :]
                    if kind == "v":
                        v.wait_ge(ring_full, b0("ring_full") + n + 1)
                        nc.vector.tensor_copy(v_rows[:, 2 * i:2 * i + 2, 0:VW],
                                              ps[:, 0:2 * VW].rearrange("p (r c) -> p r c", r=2)).then_inc(ring_free, 1)
                    else:
                        hi, lo = (q_hi, q_lo) if kind == "q" else (k_hi, k_lo)
                        c = slice(h * BANK, (h + 1) * BANK)
                        v.wait_ge(ring_hi, b0("ring_hi") + n + 1)
                        nc.vector.scalar_tensor_tensor(out=lo[:, i, c], in0=ps, scalar=vcol(f"s{idx}_b{kind}", i),
                                                       in1=hi[:, i, c].bitcast(F32), op0=ALU.add,
                                                       op1=ALU.subtract).then_inc(ring_free, 1)
                v.wait_ge(win_zero, b0("win_zero") + 1)
                v.wait_ge(ring_free, b0("ring_free") + len(jobs))
                v.wait_ge(m_ld, b0("m_ld") + 16 * ((B if per_batch else 1) + 1 + (idx == 0)))
                if not additive:
                    v.wait_ge(ma_ready, b0("ma_ready") + 1)
                with v.Fori(0, 2) as m:
                    v.wait_ge(score_done, m * U + (b0("score_done") + 1))
                    for tt in range(RT):
                        x = nc.vector.tensor_scalar(
                            v_win[:, tt, PAD:PAD + NV * P].rearrange("p (h c) -> p h c", c=P)[:, :, 0:HD],
                            v_rows[:, tt, bass.ds(m * (NV * HD), NV * HD)].rearrange("p (h c) -> p h c", c=HD),
                            1.0, None, ALU.mult)
                    x.then_inc(win_ready, 1)
                    for s in range(STEPS):
                        i = s if additive else s - 1
                        if 0 <= i < U:
                            if i >= 3:
                                v.wait_ge(exp_done, m * U + (b0("exp_done") + i - 2))
                            if additive:
                                v.wait_ge(score_done, m * U + (b0("score_done") + i + 1))
                            else:
                                v.wait_ge(mul_done, m * U + (b0("mul_done") + i + 1))
                        e = s - LC
                        if 0 <= e < U and evac_on_v(e):
                            v.wait_ge(turn_done, m * U + (b0("turn_done") + e + 1))
                            if e >= 3:
                                v.wait_ge(pv_done, m * U + (b0("pv_done") + e - 2))
                            nc.vector.tensor_copy(pt[:, e % 3, :], PS[:, 2 + e % 2, :]).then_inc(pt_v, 1)
                        elif 0 <= i < U:
                            nc.vector.memset(pace[:, s % 8:s % 8 + 1], 0.0)
                        if 0 <= i < U:
                            g, b, j = unit[i]
                            for qt in range(2):
                                c = slice(qt * S, (qt + 1) * S)
                                in0 = PS[:, i % 2, c] if additive else smul[:, i % 2, c]
                                add = mask if additive else mask_add
                                x = nc.vector.tensor_tensor_reduce(sm[:, i % 3, c], in0, add[:, b if per_batch else 0, qt, :],
                                                                   -1.0, 3.0e38, ALU.add, ALU.min,
                                                                   nmax[:, i % 4, qt:qt + 1])
                            x.then_inc(max_done, 1)
                        if not additive and s < U:
                            g, b, j = unit[s]
                            v.wait_ge(score_done, m * U + (b0("score_done") + s + 1))
                            if s >= 2:
                                v.wait_ge(max_done, m * U + (b0("max_done") + s - 1))
                            nc.vector.tensor_tensor(smul[:, s % 2, :], PS[:, s % 2, :],
                                                    mask[:, b if per_batch else 0].rearrange("p r n -> p (r n)"),
                                                    ALU.mult).then_inc(mul_done, 1)
                        for b in range(B):
                            if s == last[b] + LX + 1:
                                v.wait_ge(exp_done, m * U + (b0("exp_done") + last[b] + 1))
                                nc.vector.reciprocal(rsum[:, b, :, 0:heads_t], sums[:, b, :, 0:heads_t]).then_inc(rs_done, 1)
                            if s == last[b] + LV + 1:
                                v.wait_ge(rx_copied, m * B + (b0("rx_copied") + b + 1))
                                nc.vector.tensor_tensor(of_sb[:, b % 2, :], PS[:, 4 + b, 0:S], rx_sb[:, b % 2, :],
                                                        ALU.mult).then_inc(o_mul, 1)
                                v.wait_ge(o_mul, m * B + (b0("o_mul") + b + 1))
                                oh = q_hi[:, bass.ds(m, 1), b * S:(b + 1) * S].rearrange("p a n -> p (a n)")
                                ol = q_lo[:, bass.ds(m, 1), b * S:(b + 1) * S].rearrange("p a n -> p (a n)")
                                bv = vec[:, bass.ds(m + VEC.at[f"s{idx}_bv"], 1)]
                                nc.vector.tensor_scalar(oh, of_sb[:, b % 2, :], bv, None, ALU.add).then_inc(o_hi, 1)
                                v.wait_ge(o_hi, m * B + (b0("o_hi") + b + 1))
                                nc.vector.scalar_tensor_tensor(out=ol, in0=of_sb[:, b % 2, :], scalar=bv,
                                                               in1=oh.bitcast(F32), op0=ALU.add,
                                                               op1=ALU.subtract).then_inc(o_ready, 1)
                v.wait_ge(xb_ready, b0("xb_ready") + 1)
                for n in range(4):
                    v.wait_ge(ring_full, b0("ring_full") + len(jobs) + n + 1)
                    nc.vector.tensor_tensor(X[:, 2 * n:2 * n + 2, :].rearrange("p r d -> p (r d)"), PS[:, n, :],
                                            X[:, 2 * n:2 * n + 2, :].rearrange("p r d -> p (r d)"),
                                            ALU.add).then_inc(ring_free, 1)
                    v.wait_ge(ring_free, b0("ring_free") + len(jobs) + n + 1)
                    tile_stats((2 * n, 2 * n + 1))

        def add(name, k):
            count[name] = count.get(name, 0) + k

        for nm in ("ring_full", "ring_free"):
            add(nm, len(jobs) + 4)
        add("ring_hi", V0)
        add("m_ld", 16 * ((B if per_batch else 1) + 1 + (idx == 0)))
        add("stack_ld", 256)
        for nm in ("win_zero", "xb_ready"):
            add(nm, 1)
        add("ma_ready", 0 if additive else 1)
        add("win_ready", 2)
        for nm in ("score_done", "max_done", "exp_done", "turn_done", "pv_done"):
            add(nm, 2 * U)
        add("mul_done", 0 if additive else 2 * U)
        add("pt_v", 2 * NV_M)
        add("pt_a", 2 * NA_M)
        for nm in ("rs_done", "rt_done", "rt_copied", "rx_done", "rx_copied", "o_mul", "o_hi", "o_ready"):
            add(nm, 2 * B)

    def ln_block(eps, scale, shift, load, act, pool):
        base = dict(count)

        def b0(name):
            return base.get(name, 0)

        with nc.Block() as block:

            @block.vector
            def _(v):
                ln_stats(v, b0("ln_step"), eps, b0("ln_sqrt") + 1)
                ln_normalise(v, xn)
                affine_dve(v, all_banks, b0("ring_free"), 0, b0("h_ready"), lambda dt: vcol(scale, dt),
                           lambda dt: vcol(shift, dt))

            @block.scalar
            def _(a):
                ln_root(a, b0("ln_step"))
                act(a)
                affine_act(a, b0("ring_free"), 0, b0("h_ready"))

            @block.sync
            def _(sp):
                load(sp)

            @block.gpsimd
            def _(p):
                pool(p)

            @block.tensor
            def _(t):
                turn_pe(t, xn, all_banks, b0("ring_free"), 0, b0("xn_ready"))

        for nm, k in (("ln_step", LN_STEPS), ("ln_sqrt", 1), ("xn_ready", RT), ("ring_full", 4), ("ring_free", 4),
                      ("h_ready", 4), ("hf_hi", 4)):
            count[nm] = count.get(nm, 0) + k

    g_act = sem("g_act")
    g_ready = sem("g_ready")
    mw_ld = sem("mw_ld")
    mw_hi = sem("mw_hi")
    mw_lo = sem("mw_lo")
    b2_added = sem("b2_added")
    G_JOBS = FT * HALF

    def mlp_pe(t, bank_of, br, first, mw, bg, w1h, w1l, w2h, w2l, gh, gl):
        for j in range(G_JOBS):
            n = first + j
            f, h = divmod(j, HALF)
            t.wait_ge(ring_free, br + n - len(bank_of) + 1) if first or n >= len(bank_of) else None
            if j == 0:
                t.wait_ge(mw_lo, mw + 1)
            k = 0
            for dt in range(DT):
                c = slice(h * BANK, (h + 1) * BANK)
                w = slice(f * P, (f + 1) * P)
                for lhs, rhs in hi_passes(w1h[:, dt, w], w1l[:, dt, w], h_hi[:, dt, c], h_lo[:, dt, c]):
                    mm = nc.tensor.matmul(PS[:, bank_of[n % len(bank_of)], :], lhs, rhs, start=(k == 0), stop=(k == 5))
                    k += 1
            mm.then_inc(ring_full, 1)
        for j in range(RT // 2):
            n = first + G_JOBS + j
            t.wait_ge(ring_free, br + n - len(bank_of) + 1)
            if j == 0:
                t.wait_ge(mw_lo, mw + 2)
                t.wait_ge(g_ready, bg + G_JOBS)
            for r in range(2):
                c = slice((2 * j + r) * P, (2 * j + r + 1) * P)
                k = 0
                for f in range(FT):
                    for lhs, rhs in hi_passes(gh[:, f, c], gl[:, f, c], w2h[:, f, :], w2l[:, f, :]):
                        mm = nc.tensor.matmul(PS[:, bank_of[n % len(bank_of)], r * D:(r + 1) * D], lhs, rhs,
                                              start=(k == 0), stop=(k == 3 * FT - 1))
                        k += 1
            mm.then_inc(ring_full, 1)

    def mlp_split_act(a, ld, wst1, wst2, w1h, w2h):
        a.wait_ge(mw_ld, ld + 48)
        nc.scalar.activation(w1h[:], wst1[:], ACT.Copy).then_inc(mw_hi, 1)
        nc.scalar.activation(w2h[:], wst2[:], ACT.Copy).then_inc(mw_hi, 1)

    def mlp_act(a, bank_of, br, first, bg, func, b1):
        for j in range(G_JOBS):
            n = first + j
            a.wait_ge(ring_full, br + n + 1)
            if j >= 2:
                a.wait_ge(g_ready, bg + j - 1)
            nc.scalar.activation(hf[:, j % 2, :], PS[:, bank_of[n % len(bank_of)], :], func,
                                 bias=b1(j // HALF)).then_inc(g_act, 1)

    def mlp_pool(p, mw, bx, wst1, wst2, w1h, w1l, w2h, w2l, b2_row):
        for i, (st, h, lo) in enumerate(((wst1, w1h, w1l), (wst2, w2h, w2l))):
            p.wait_ge(mw_hi, mw + i + 1)
            nc.gpsimd.tensor_tensor(lo[:], st[:], h[:].bitcast(F32), ALU.subtract).then_inc(mw_lo, 1)
            if i == 0:
                p.wait_ge(xn_ready, bx)
                nc.gpsimd.tensor_tensor(X[:], X[:], b2_row[:].unsqueeze(1).to_broadcast([P, RT, D]),
                                        ALU.add).then_inc(b2_added, 1)

    def mlp_dve(v, bank_of, br, first, bg, bb, gh, gl):
        for j in range(G_JOBS + 1):
            if j < G_JOBS:
                f, h = divmod(j, HALF)
                c = slice(h * BANK, (h + 1) * BANK)
                v.wait_ge(g_act, bg + j + 1)
                nc.vector.tensor_copy(gh[:, f, c], hf[:, j % 2, :]).then_inc(ring_free, 1)
            if j >= 1:
                f, h = divmod(j - 1, HALF)
                c = slice(h * BANK, (h + 1) * BANK)
                v.wait_ge(ring_free, br + first + j)
                nc.vector.tensor_tensor(gl[:, f, c], hf[:, (j - 1) % 2, :], gh[:, f, c].bitcast(F32),
                                        ALU.subtract).then_inc(g_ready, 1)
        v.wait_ge(b2_added, bb + 1)
        for j in range(RT // 2):
            n = first + G_JOBS + j
            v.wait_ge(ring_full, br + n + 1)
            xr = X[:, 2 * j:2 * j + 2, :].rearrange("p r d -> p (r d)")
            nc.vector.tensor_tensor(xr, PS[:, bank_of[n % len(bank_of)], :], xr, ALU.add).then_inc(ring_free, 1)
            v.wait_ge(ring_free, br + n + 1)
            nc.vector.memset(newt[:, 0:1], 0.0)
            tile_stats((2 * j, 2 * j + 1))

    small_attention(0, 8, True, ctx_hi, ctx_lo, io["mask0"], True)

    base0 = dict(count)
    with nc.Block() as block:

        @block.sync
        def _(sp):
            for i, nm in enumerate(("gamma", "beta")):
                sp.dma_start(gb_rows[:, i, :], io[nm].to_broadcast([P, D])).then_inc(m_ld, 16)

        @block.scalar
        def _(a):
            ln_root(a, base0.get("ln_step", 0))

        @block.vector
        def _(v):
            ln_stats(v, base0.get("ln_step", 0), 1e-6, base0.get("ln_sqrt", 0) + 1)
            ln_normalise(v, xn)
            v.wait_ge(m_ld, base0["m_ld"] + 32)
            v.wait_ge(xn_ready, base0.get("xn_ready", 0) + RT)
            nc.vector.tensor_tensor(X[:], xn[:], gb_rows[:, 0:1, :].to_broadcast([P, RT, D]),
                                    ALU.mult).then_inc(ln_step, 1)
            v.wait_ge(ln_step, base0.get("ln_step", 0) + LN_STEPS + 1)
            nc.vector.tensor_tensor(X[:], X[:], gb_rows[:, 1:2, :].to_broadcast([P, RT, D]),
                                    ALU.add).then_inc(ln_step, 1)
            v.wait_ge(ln_step, base0.get("ln_step", 0) + LN_STEPS + 2)
            tile_stats(range(RT))

    for nm, k in (("ln_step", LN_STEPS + 2), ("ln_sqrt", 1), ("xn_ready", RT), ("m_ld", 32)):
        count[nm] = count.get(nm, 0) + k

    def small_ln(n, idx):
        ln_block(1e-5, f"L1_ln{n}_s", f"L1_ln{n}_b", lambda sp: weights_load(sp, idx), lambda a: weights_act(a, idx),
                 lambda p: weights_pool(p, idx))
        weights_count()

    small_ln(1, 1)
    small_attention(1, 16, False, h_hi, h_lo, io["ltor"], False)
    small_ln(2, 2)
    small_attention(2, 16, False, ctx_hi, ctx_lo, io["cross"], True)

    def small_mlp_load(sp):
        sp.dma_start(mws1[:], io["s_w1"].rearrange("(t p) n -> p t n", p=P)).then_inc(mw_ld, 16)
        sp.dma_start(mws2[:], io["s_w2"].rearrange("(t p) n -> p t n", p=P)).then_inc(mw_ld, 16)
        sp.dma_start(b2s_row[:], io["s_b2"].to_broadcast([P, D])).then_inc(mw_ld, 16)

    ln_block(1e-5, "L1_ln3_s", "L1_ln3_b", small_mlp_load, lambda a: mlp_split_act(a, 0, mws1, mws2, mw1h, mw2h),
             lambda p: mlp_pool(p, 0, now("xn_ready") + RT, mws1, mws2, mw1h, mw1l, mw2h, mw2l, b2s_row))
    for nm, k in (("mw_ld", 48), ("mw_hi", 2), ("mw_lo", 2), ("b2_added", 1)):
        count[nm] = count.get(nm, 0) + k

    bm = dict(count)
    with nc.Block() as block:

        @block.tensor
        def _(t):
            mlp_pe(t, all_banks, bm["ring_free"], 0, 0, 0, mw1h, mw1l, mw2h, mw2l, gs_hi, gs_lo)

        @block.scalar
        def _(a):
            mlp_act(a, all_banks, bm["ring_full"], 0, 0, ACT.Gelu_apprx_tanh, lambda f: vcol("L1_b1", f))

        @block.vector
        def _(v):
            mlp_dve(v, all_banks, bm["ring_free"], 0, 0, 0, gs_hi, gs_lo)

    for nm, k in (("ring_full", G_JOBS + 4), ("ring_free", G_JOBS + 4), ("g_act", G_JOBS), ("g_ready", G_JOBS)):
        count[nm] = count.get(nm, 0) + k
    small.close()
    big = ExitStack()
    xnb = sbt(big, "xnb", [P, RT, D])
    stage = {k: sbt(big, f"stage_{k}", [P, 2, 2 * BK]) for k in "qkvo"}
    pb = sbt(big, "pb", [P, 2, 2, KC])
    bc = sbt(big, "bc", [P, 2, HEADV])
    bcm = sbt(big, "bcm", [P, FT])
    nmaxb = sbt(big, "nmaxb", [P, 2, 2])
    sumb = sbt(big, "sumb", [P, 2, 2])
    rsb = sbt(big, "rsb", [P, 2, 2])
    p_key = sbt(big, "p_key", [P, RT, P])
    v_key = sbt(big, "v_key", [P, BH, BH + 1])
    v_cur = sbt(big, "v_cur", [P, 2, BH + 1])
    r_key = sbt(big, "r_key", [P, D])
    bo_all = sbt(big, "bo_all", [1, 4, D])
    bo_cur = sbt(big, "bo_cur", [1, D])
    e_last = sbt(big, "e_last", [1, BH + 1])
    b2_row = sbt(big, "b2_row", [P, D])
    mst1 = sbt(big, "mst1", [P, DT, F])
    mst2 = sbt(big, "mst2", [P, FT, D])
    scope_a = ExitStack()
    kT = [[sbt(scope_a, f"kT{x}_{y}", [P, B, KC], F32R) for y in ("hi", "lo")] for x in range(2)]
    qT = [[sbt(scope_a, f"qT{x}_{y}", [P, N], F32R) for y in ("hi", "lo")] for x in range(2)]
    vr = [sbt(scope_a, f"vr_{y}", [P, RT, 2 * BK], F32R) for y in ("hi", "lo")]
    oT = [[sbt(scope_a, f"oT{x}_{y}", [P, N], F32R) for y in ("hi", "lo")] for x in range(2)]
    wsp = {k: [sbt(scope_a, f"w{k}_{y}", [P, 2, 2 * BK], F32R) for y in ("h", "l")] for k in "qkvo"}
    pT = [sbt(scope_a, f"pT_{y}", [P, 4, BANK], F32R) for y in ("hi", "lo")]
    scope_a.close()
    scope_m = ExitStack()
    gb_hi = sbt(scope_m, "gb_hi", [P, FT, N], F32R)
    gb_lo = sbt(scope_m, "gb_lo", [P, FT, N], F32R)
    bw1h = sbt(scope_m, "bw1h", [P, DT, F], F32R)
    bw1l = sbt(scope_m, "bw1l", [P, DT, F], F32R)
    bw2h = sbt(scope_m, "bw2h", [P, FT, D], F32R)
    bw2l = sbt(scope_m, "bw2l", [P, FT, D], F32R)
    scope_m.close()
    assert ATT_W * 4 + VEC.at["att"] <= VEC.n

    s_ld = {k: sem(f"stage_ld_{k}") for k in "qkvo"}
    s_hi = {k: sem(f"split_hi_{k}") for k in "qkvo"}
    s_lo = {k: sem(f"split_lo_{k}") for k in "qkvo"}
    bc_ready = sem("bc_ready")
    rec_done = sem("rec_done")
    norm_done = sem("norm_done")
    key_done = sem("key_done")
    pt_hi = sem("pt_hi")
    pt_lo = sem("pt_lo")
    vk_step = sem("vk_step")
    v_cur_ready = sem("v_cur_ready")
    setup_done = sem("setup_done")
    bo_ld = sem("bo_ld")

    RING = [5, 6, 7]
    NR = len(RING)

    def ring_bank(n):
        return PS[:, RING[n % NR], :]

    def ring_from(n):
        return [RING[(n + i) % NR] for i in range(NR)]

    PT0 = 1
    UA = B * BH
    PRO = [("k", 0, 0), ("k", 0, 1)] + ["turn"] * 4 + [("q", 0, 0), ("q", 0, 1)]
    STEP = [
        [("k", 1, 0), ("v", 0), ("v", 1)],
        [("k", 1, 1), ("pv", 1, 1)],
        [("q", 1, 0), ("o", 0), ("o", 1)],
        [("q", 1, 1), ("pv", 0, 0), ("v", 2)],
        [("v", 3), ("o", 2), ("o", 3)],
        [("k", 0, 0), ("pv", 0, 1)],
        [("k", 0, 1), ("q", 0, 0), ("key",)],
        [("q", 0, 1), ("pv", 1, 0)],
    ]

    def jobs_of(step, first, last):
        js = []
        for j in STEP[step]:
            if first and (j[0] == "o" or j == ("pv", 1, 1)):
                continue
            if last and step >= 5 and j[0] in "kq" and j[0] != "key":
                continue
            js.append(j)
        return js

    def n_jobs(first, last, kinds=None, until=8):
        return sum(kinds is None or j[0] in kinds for s_ in range(until) for j in jobs_of(s_, first, last))

    def job_at(job, first, last):
        return [j for s_ in range(8) for j in jobs_of(s_, first, last)].index(job)

    HI = ("k", "q", "v", "pv")
    J_FIRST, J_MID, J_LAST = n_jobs(True, False), n_jobs(False, False), n_jobs(False, True)
    H_FIRST, H_MID = n_jobs(True, False, HI), n_jobs(False, False, HI)
    TAIL = [("pv", 1, 1), ("turnkey", 0), ("turnkey", 1)] + [("o", b) for b in range(B)]
    R_ATT = len(PRO) + J_FIRST + 6 * J_MID + J_LAST + len(TAIL)
    H_ATT = 2 * 8 + 2 * 8 + 2 * 8 + 4 * 8 + 0
    H_ATT = 4 + H_FIRST + 6 * H_MID + n_jobs(False, True, HI) + 1
    R_LAYER = 2 * R_ATT + 4 + G_JOBS + 4
    bb_ = dict(count)
    assert R_LAYER % NR == 0 and 2 * J_MID % NR == 0

    def c0(name):
        return bb_.get(name, 0)

    class At:

        def __init__(self, l, a):
            self.ring = l * R_LAYER + (a * R_ATT + c0("ring_full"))
            self.hi = l * (2 * H_ATT) + (a * H_ATT + c0("ring_hi"))
            self.unit = l * (2 * UA) + a * UA
            self.pair = l * (2 * PAIRS) + a * PAIRS
            self.bc = l * (4 * PAIRS) + 2 * a * PAIRS
            self.lns = l * 3 + a
            self.vk = l * (2 * VK_STEPS) + a * VK_STEPS
            self.vec = l * (2 * ATT_W) + (a * ATT_W + VEC.at["att"])
            self.a = a
            self.l = l

        def pair_ring(self, p, first):
            return self.ring + len(PRO) if first else self.ring + (len(PRO) + J_FIRST) + (p - 1) * J_MID

        def pair_hi(self, p, first):
            return self.hi + 4 if first else self.hi + (4 + H_FIRST) + (p - 1) * H_MID

    VK_STEPS = 6

    def each_pair(eng, at, body):
        par = (c0("ring_full") + at.a * R_ATT + len(PRO)) % NR
        body(at, 0, True, False, par)
        par = (par + J_FIRST) % NR
        with eng.Fori(0, (PAIRS - 2) // 2) as i:
            body(at, i * 2 + 1, False, False, par)
            body(at, i * 2 + 2, False, False, (par + J_MID) % NR)
        body(at, PAIRS - 1, False, True, par)

    with nc.Block() as block:

        @block.sync
        def _(sp):
            sp.dma_start(bo_all[:], io["bo"].rearrange("(o a) d -> o a d", o=1)).then_inc(bo_ld, 16)
            names = {"k": io["wk"], "q": io["wq"], "v": io["wv"], "o": io["wo"]}

            def load(att, p, kind):
                w = names[kind]
                if kind == "o":
                    src = w[bass.ds(att, 1), bass.ds(p * (2 * BK), 2 * BK), :].rearrange("a (t p) n -> p (a t) n", p=P)
                else:
                    src = w[bass.ds(att, 1), :, bass.ds(p * (2 * BK), 2 * BK)].rearrange("a (t p) n -> p (a t) n", p=P)
                sp.dma_start(stage[kind][:], src).then_inc(s_ld[kind], 16)

            def mlp_load(l, wait):
                if wait:
                    sp.wait_ge(mw_lo, c0("mw_lo") + 2)
                    sp.wait_ge(b2_added, c0("b2_added") + 1)
                sp.dma_start(mst1[:], io["w1"][l].rearrange("(t p) n -> p t n", p=P)).then_inc(mw_ld, 16)
                sp.dma_start(mst2[:], io["w2"][l].rearrange("(t p) n -> p t n", p=P)).then_inc(mw_ld, 16)
                sp.dma_start(b2_row[:], io["b2"][l:l + 1, :].to_broadcast([P, D])).then_inc(mw_ld, 16)

            for kind in "kqvo":
                load(0, 0, kind)
            mlp_load(0, False)
            with sp.Fori(1, PAIRS) as p:
                for kind in "kqvo":
                    sp.wait_ge(s_lo[kind], p)
                    load(0, p, kind)
            with sp.Fori(1, 4) as att:
                with sp.Fori(0, PAIRS) as p:
                    for kind in "kqvo":
                        sp.wait_ge(s_lo[kind], att * PAIRS + p)
                        load(att, p, kind)
            mlp_load(1, True)

        @block.tensor
        def _(t):
            def take(n):
                t.wait_ge(ring_free, n - (NR - 1))

            def body(at, p, first, last, bank0):
                rb = at.pair_ring(p, first)
                u0 = at.unit + p * 8
                k = 0

                def job(j):
                    nonlocal k
                    n = rb + k
                    take(n)
                    ps = ring_bank(bank0 + k)
                    k += 1
                    run_job(t, at, j, p, ps, rb, first, last)

                for s in range(8):
                    x, b = divmod(s, 4)
                    sl = s % 2
                    if x == 0 and b in (0, 2):
                        if first:
                            if b == 0:
                                t.wait_ge(ring_free, at.ring + len(PRO))
                        else:
                            t.wait_ge(ring_free, rb - (n_jobs(False, False) - job_at(("q", 0, b // 2), False, False)) + 1)
                    elif x == 1 and b in (0, 2):
                        t.wait_ge(ring_free, rb + (job_at(("q", 1, b // 2), first, last) + 1))
                    t.wait_ge(exp_done, u0 + (c0("exp_done") + s - 1))
                    for qt in range(2):
                        i = 0
                        c = slice(b * S + qt * P, b * S + (qt + 1) * P)
                        for lhs, rhs in hi_passes(qT[x][0][:, c], qT[x][1][:, c], kT[x][0][:, b, :], kT[x][1][:, b, :]):
                            mm = nc.tensor.matmul(PS[:, 2 * sl + qt, 0:KC], lhs, rhs, start=(i == 0), stop=(i == 2))
                            i += 1
                    mm.then_inc(score_done, 1)
                    if not (first and s == 0):
                        turn_unit(t, u0 + s - 1, (s - 1) % 8)
                    for j in jobs_of(s, first, last):
                        job(j)
                return rb + k

            def turn_unit(t, u, s):
                t.wait_ge(norm_done, u + 1)
                t.wait_ge(pt_lo, u + PT0)
                for tt in range(2):
                    for qt in range(2):
                        mm = nc.tensor.transpose(PS[:, 4, tt * S + qt * P:tt * S + (qt + 1) * P],
                                                 pb[:, s % 2, qt, tt * P:(tt + 1) * P], ident[:])
                mm.then_inc(turn_done, 1)

            def run_job(t, at, j, p, ps, rb, first, last):
                kind = j[0]
                if kind in ("k", "q"):
                    _, x, h = j
                    nxt = x == 0
                    if h == 0:
                        t.wait_ge(s_lo[kind], at.pair + (p + (2 if nxt else 1)))
                        if kind == "q":
                            pass
                    project(t, kind, x, h, ps)
                elif kind == "v":
                    b = j[1]
                    if b == 0:
                        t.wait_ge(s_lo["v"], at.pair + (p + 1))
                    for r in range(2):
                        i = 0
                        c = slice((2 * b + r) * P, (2 * b + r + 1) * P)
                        for dt in range(DT):
                            for lhs, rhs in hi_passes(ctx_hi[:, dt, c], ctx_lo[:, dt, c],
                                                      wsp["v"][0][:, dt, :], wsp["v"][1][:, dt, :]):
                                mm = nc.tensor.matmul(ps[:, r * S:(r + 1) * S], lhs, rhs, start=(i == 0), stop=(i == 5))
                                i += 1
                    mm.then_inc(ring_full, 1)
                elif kind == "pv":
                    _, x, half = j
                    if x == 0:
                        t.wait_ge(ring_free, rb + (job_at(("v", 2 * half + 1), first, last) + 1))
                    pv_job(t, at, p, x, half, ps, at.unit)
                elif kind == "o":
                    if j[1] == 0:
                        t.wait_ge(ring_free, rb + (job_at(("pv", 1, 1), first, last) + 1))
                    o_job(t, at, j[1], ps, at.pair + p, False)
                elif kind == "key":
                    t.wait_ge(s_ld["o"], (at.pair + (p + 1)) * 16)
                    t.wait_ge(v_cur_ready, at.pair + (p + 1))
                    for x in range(2):
                        mm = nc.tensor.matmul(ps[0:BH + 1, 0:D], v_cur[:, x, :], stage["o"][:, x, :],
                                              start=(x == 0), stop=(x == 1 and not isinstance(p, int)) or
                                              (x == 1 and p != 0))
                    if isinstance(p, int) and p == 0:
                        mm = nc.tensor.matmul(ps[0:BH + 1, 0:D], e_last[:], bo_cur[:], start=False, stop=True)
                    mm.then_inc(ring_full, 1)

            def project(t, kind, x, h, ps):
                i = 0
                c = slice(h * BANK, (h + 1) * BANK)
                w = slice(x * BK, (x + 1) * BK)
                xh, xl = (h_hi, h_lo) if kind == "q" else (ctx_hi, ctx_lo)
                for dt in range(DT):
                    for lhs, rhs in hi_passes(wsp[kind][0][:, dt, w], wsp[kind][1][:, dt, w], xh[:, dt, c], xl[:, dt, c]):
                        mm = nc.tensor.matmul(ps, lhs, rhs, start=(i == 0), stop=(i == 5))
                        i += 1
                mm.then_inc(ring_full, 1)

            def pv_job(t, at, p, x, half, ps, unit0):
                for r in range(2):
                    b = 2 * half + r
                    s = 4 * x + b
                    back = 8 if (x == 1 and half == 1) else 0
                    t.wait_ge(pt_lo, unit0 + (p * 8 + (PT0 + s - back + 1)))
                    i = 0
                    for tt in range(2):
                        for lhs, rhs in hi_passes(vr[0][:, 2 * b + tt, x * BK:(x + 1) * BK],
                                                  vr[1][:, 2 * b + tt, x * BK:(x + 1) * BK],
                                                  pT[0][:, s % 4, tt * S:(tt + 1) * S], pT[1][:, s % 4, tt * S:(tt + 1) * S]):
                            mm = nc.tensor.matmul(ps[:, r * S:(r + 1) * S], lhs, rhs, start=(i == 0), stop=(i == 5))
                            i += 1
                mm.then_inc(ring_full, 1)

            def o_job(t, at, b, ps, w_pair, with_key):
                if b == 0:
                    t.wait_ge(s_lo["o"], w_pair)
                for r in range(2):
                    c = slice((2 * b + r) * P, (2 * b + r + 1) * P)
                    i = 0
                    for x in range(2):
                        for lhs, rhs in hi_passes(oT[x][0][:, c], oT[x][1][:, c], wsp["o"][0][:, x, :], wsp["o"][1][:, x, :]):
                            mm = nc.tensor.matmul(ps[:, r * D:(r + 1) * D], lhs, rhs, start=(i == 0),
                                                  stop=(i == 5 and not with_key))
                            i += 1
                    if with_key:
                        mm = nc.tensor.matmul(ps[:, r * D:(r + 1) * D],
                                              hf[:, b // 2, (b % 2) * S + r * P:(b % 2) * S + (r + 1) * P], r_key[:],
                                              start=False, stop=True)
                mm.then_inc(ring_full, 1)

            def attention(l, a):
                at = At(l, a)
                par = (c0("ring_full") + a * R_ATT) % NR
                for n, j in enumerate(PRO):
                    ps = ring_bank(par + n)
                    if j == "turn":
                        h, dt = TURNS[n - 2]
                        t.wait_ge(xn_ready, at.lns * RT + (c0("xn_ready") + 4 * h + 4))
                        take(at.ring + n)
                        for r in range(4):
                            mm = nc.tensor.transpose(ps[:, r * P:(r + 1) * P], xnb[:, 4 * h + r, dt * P:(dt + 1) * P], ident[:])
                        mm.then_inc(ring_full, 1)
                    else:
                        t.wait_ge(s_lo[j[0]], at.pair + 1)
                        if j[0] == "q":
                            t.wait_ge(h_ready, at.lns * 4 + (c0("h_ready") + 4))
                        take(at.ring + n)
                        project(t, j[0], j[1], j[2], ps)
                each_pair(t, at, body)
                turn_unit(t, at.unit + UA - 1, 7)
                base = at.ring + (R_ATT - len(TAIL))
                par = (c0("ring_full") + a * R_ATT + R_ATT - len(TAIL)) % NR
                for n, j in enumerate(TAIL):
                    ps = ring_bank(par + n)
                    take(base + n)
                    if j[0] == "pv":
                        pv_job(t, at, PAIRS, 1, 1, ps, at.unit)
                    elif j[0] == "turnkey":
                        if j[1] == 0:
                            t.wait_ge(key_done, at.unit + UA)
                        for r in range(4):
                            mm = nc.tensor.transpose(ps[:, r * P:(r + 1) * P], p_key[:, 4 * j[1] + r, :], ident[:])
                        mm.then_inc(ring_full, 1)
                    else:
                        t.wait_ge(ring_free, base + 3)
                        o_job(t, at, j[1], ps, at.pair + PAIRS, True)

            with t.Fori(0, 2) as l:
                attention(l, 0)
                attention(l, 1)
                at = At(l, 2)
                par = (c0("ring_full") + 2 * R_ATT) % NR
                for n, (h, dt) in enumerate(TURNS):
                    ps = ring_bank(par + n)
                    t.wait_ge(xn_ready, at.lns * RT + (c0("xn_ready") + 4 * h + 4))
                    take(at.ring + n)
                    for r in range(4):
                        mm = nc.tensor.transpose(ps[:, r * P:(r + 1) * P], xnb[:, 4 * h + r, dt * P:(dt + 1) * P], ident[:])
                    mm.then_inc(ring_full, 1)
                t.wait_ge(h_ready, at.lns * 4 + (c0("h_ready") + 4))
                mlp_pe(t, ring_from(par), at.ring, 4, l * 2 + c0("mw_lo"), l * G_JOBS + c0("g_ready"),
                       bw1h, bw1l, bw2h, bw2l, gb_hi, gb_lo)

        @block.scalar
        def _(a_):
            def split(at_pair, kind):
                a_.wait_ge(s_ld[kind], at_pair * 16)
                nc.scalar.activation(wsp[kind][0][:], stage[kind][:], ACT.Copy).then_inc(s_hi[kind], 1)

            def hi_job(at, j, n, ps):
                kind = j[0]
                a_.wait_ge(ring_full, n + 1)
                if kind in ("k", "q"):
                    _, x, h = j
                    if kind == "k":
                        nc.scalar.activation(kT[x][0][:, 2 * h:2 * h + 2, 0:S], ps.rearrange("p (b n) -> p b n", b=2),
                                             ACT.Identity, bias=bc[:, x, 1:2])
                        nc.scalar.activation(kT[x][0][:, 2 * h:2 * h + 2, S:KC],
                                             bc[:, x, 2:3].unsqueeze(1).to_broadcast([P, 2, 2]),
                                             ACT.Copy).then_inc(ring_hi, 1)
                    else:
                        nc.scalar.activation(qT[x][0][:, h * BANK:(h + 1) * BANK], ps, ACT.Identity,
                                             bias=bc[:, x, 0:1]).then_inc(ring_hi, 1)
                elif kind == "v":
                    b = j[1]
                    nc.scalar.activation(vr[0][:, 2 * b:2 * b + 2, :].rearrange("p r n -> p (r n)"), ps,
                                         ACT.Copy).then_inc(ring_hi, 1)
                else:
                    _, x, half = j
                    nc.scalar.activation(oT[x][0][:, half * BANK:(half + 1) * BANK], ps, ACT.Copy).then_inc(ring_hi, 1)

            def turned(u, s):
                a_.wait_ge(turn_done, u + (c0("turn_done") + 1))
                nc.scalar.activation(pT[0][:, s % 4, :], PS[:, 4, :], ACT.Copy).then_inc(pt_hi, 1)

            def body(at, p, first, last, bank0):
                rb = at.pair_ring(p, first)
                u0 = at.unit + p * 8
                k = 0
                for s in range(8):
                    sl = s % 2
                    js = jobs_of(s, first, last)
                    if not (first and s == 0):
                        turned(u0 + s - 1, (s - 1) % 8)
                    a_.wait_ge(max_done, u0 + (c0("max_done") + s + 1))
                    a_.wait_ge(turn_done, u0 + (c0("turn_done") + s - 1))
                    for qt in range(2):
                        e = nc.scalar.activation(pb[:, sl, qt, 0:S + 1], PS[:, 2 * sl + qt, 0:S + 1], ACT.Exp,
                                                 bias=nmaxb[:, sl, qt:qt + 1], accum_out=sumb[:, sl, qt:qt + 1])
                    e.then_inc(exp_done, 1)
                    for j in js:
                        if j[0] in HI:
                            if j[0] in ("k", "q") and j[2] == 0:
                                a_.wait_ge(bc_ready, at.bc + (p * 2 + (2 if j[1] == 1 else 3)))
                            hi_job(at, j, rb + k, ring_bank(bank0 + k))
                        k += 1
                    if not last:
                        nxt = at.pair + (p + 2)
                        if s == 2:
                            split(nxt, "k")
                        if s == 4:
                            split(nxt, "q")
                        if s == 5:
                            split(nxt, "v")
                    if s == 7:
                        a_.wait_ge(ring_full, rb + n_jobs(first, last, until=7))
                        split(at.pair + (p + 1), "o")

            def attention(l, a):
                at = At(l, a)
                a_.wait_ge(ln_step, l * (3 * LN_STEPS) + (a * LN_STEPS + c0("ln_step") + 2 * RT + 1))
                nc.scalar.activation(rstd[:], vareps[:], ACT.Sqrt).then_inc(ln_sqrt, 1)
                split(at.pair + 1, "k")
                split(at.pair + 1, "q")
                split(at.pair + 1, "v")
                par = (c0("ring_full") + a * R_ATT) % NR
                a_.wait_ge(bc_ready, at.bc + 1)
                for n, j in enumerate(PRO):
                    ps = ring_bank(par + n)
                    if j == "turn":
                        h, dt = TURNS[n - 2]
                        a_.wait_ge(ring_free, at.ring + n + 1)
                        nc.scalar.activation(h_hi[:, dt, h * BANK:(h + 1) * BANK], hf[:, (n - 2) % 2, :],
                                             ACT.Copy).then_inc(hf_hi, 1)
                    else:
                        hi_job(at, j, at.ring + n, ps)
                each_pair(a_, at, body)
                turned(at.unit + UA - 1, 7)
                base = at.ring + (R_ATT - len(TAIL))
                par = (c0("ring_full") + a * R_ATT + R_ATT - len(TAIL)) % NR
                hi_job(at, TAIL[0], base, ring_bank(par))

            with a_.Fori(0, 2) as l:
                attention(l, 0)
                attention(l, 1)
                at = At(l, 2)
                a_.wait_ge(ln_step, l * (3 * LN_STEPS) + (2 * LN_STEPS + c0("ln_step") + 2 * RT + 1))
                nc.scalar.activation(rstd[:], vareps[:], ACT.Sqrt).then_inc(ln_sqrt, 1)
                mlp_split_act(a_, l * 48 + c0("mw_ld"), mst1, mst2, bw1h, bw2h)
                affine_act(a_, at.ring, 0, at.lns * 4 + c0("h_ready"))
                par = (c0("ring_full") + 2 * R_ATT) % NR
                mlp_act(a_, ring_from(par), at.ring, 4, l * G_JOBS + c0("g_ready"), ACT.Gelu,
                        lambda f: bcm[:, f:f + 1])

        @block.gpsimd
        def _(g):
            nc.gpsimd.memset(p_key[:], 0.0).then_inc(setup_done, 1)
            g.wait_ge(setup_done, 1)
            nc.gpsimd.memset(p_key[:, :, BH:BH + 1], 1.0).then_inc(setup_done, 1)
            nc.gpsimd.memset(r_key[:], 0.0).then_inc(setup_done, 1)
            nc.gpsimd.memset(e_last[:], 0.0).then_inc(setup_done, 1)
            nc.gpsimd.memset(v_key[:], 0.0).then_inc(setup_done, 1)
            g.wait_ge(setup_done, 5)
            nc.gpsimd.memset(e_last[:, BH:BH + 1], 1.0).then_inc(setup_done, 1)

            def split(n, kind):
                g.wait_ge(s_hi[kind], n)
                nc.gpsimd.tensor_tensor(wsp[kind][1][:], stage[kind][:], wsp[kind][0][:].bitcast(F32),
                                        ALU.subtract).then_inc(s_lo[kind], 1)

            def body(at, p, first, last, bank0):
                u0 = at.unit + p * 8
                for s in range(8):
                    x, b = divmod(s, 4)
                    sl = s % 2
                    g.wait_ge(rec_done, u0 + s + 1)
                    nc.gpsimd.tensor_tensor(p_key[:, 2 * b:2 * b + 2, bass.ds(p * 2 + x, 1)], pb[:, sl, :, S:S + 1],
                                            rsb[:, sl, :].unsqueeze(2), ALU.mult).then_inc(key_done, 1)
                    nc.gpsimd.tensor_tensor(pb[:, sl, :, 0:S], pb[:, sl, :, 0:S],
                                            rsb[:, sl, :].unsqueeze(2).to_broadcast([P, 2, S]),
                                            ALU.mult).then_inc(norm_done, 1)
                    if not last:
                        nxt = at.pair + (p + 2)
                        if s == 2:
                            split(nxt, "k")
                        if s == 4:
                            split(nxt, "q")
                        if s == 5:
                            split(nxt, "v")
                    if s == 7:
                        split(at.pair + (p + 1), "o")

            with g.Fori(0, 2) as l:
                for a in range(2):
                    at = At(l, a)
                    for kind in "kqv":
                        split(at.pair + 1, kind)
                    each_pair(g, at, body)
                at = At(l, 2)
                mlp_pool(g, l * 2 + c0("mw_hi"), at.lns * RT + (c0("xn_ready") + RT), mst1, mst2, bw1h, bw1l, bw2h, bw2l, b2_row)

        @block.vector
        def _(v):
            v.wait_ge(setup_done, 6)
            v.wait_ge(bo_ld, 16)
            nc.vector.memset(v_cur[:], 0.0).then_inc(pt_lo, PT0)

            def copy_vectors(at, h, x):
                nc.vector.tensor_scalar(bc[:, x, :], vec[:, bass.ds(at.vec + h * HEADV, HEADV)], 1.0, None,
                                        ALU.mult).then_inc(bc_ready, 1)

            def lo_job(at, j, n, hi_n, ps, p):
                kind = j[0]
                if kind in ("o", "key", "turnkey"):
                    v.wait_ge(ring_full, n + 1)
                    if kind == "o":
                        b = j[1]
                        xr = X[:, 2 * b:2 * b + 2, :].rearrange("p r d -> p (r d)")
                        v.wait_ge(ring_free, n - 3)
                        nc.vector.tensor_tensor(xr, ps, xr, ALU.add).then_inc(ring_free, 1)
                        if isinstance(p, int) and p == PAIRS:
                            v.wait_ge(ring_free, n + 1)
                            nc.vector.memset(newt[:, 0:1], 0.0)
                            tile_stats((2 * b, 2 * b + 1))
                    elif kind == "key":
                        if isinstance(p, int) and p == 0:
                            nc.vector.tensor_copy(r_key[0:BH + 1, :], ps[0:BH + 1, 0:D]).then_inc(ring_free, 1)
                        else:
                            v.wait_ge(ring_free, n - 3)
                            nc.vector.tensor_tensor(r_key[0:BH + 1, :], ps[0:BH + 1, 0:D], r_key[0:BH + 1, :],
                                                    ALU.add).then_inc(ring_free, 1)
                    else:
                        nc.vector.tensor_copy(hf[:, j[1], :], ps).then_inc(ring_free, 1)
                    return
                v.wait_ge(ring_hi, hi_n + 1)
                if kind in ("k", "q"):
                    _, x, h = j
                    if kind == "k":
                        for bb in range(2):
                            b = 2 * h + bb
                            nc.vector.scalar_tensor_tensor(out=kT[x][1][:, b, 0:S], in0=ps[:, bb * S:(bb + 1) * S],
                                                           scalar=bc[:, x, 1:2], in1=kT[x][0][:, b, 0:S].bitcast(F32),
                                                           op0=ALU.add, op1=ALU.subtract)
                        nc.vector.tensor_tensor(kT[x][1][:, 2 * h:2 * h + 2, S:KC],
                                                bc[:, x, 2:3].unsqueeze(1).to_broadcast([P, 2, 2]),
                                                kT[x][0][:, 2 * h:2 * h + 2, S:KC].bitcast(F32),
                                                ALU.subtract).then_inc(ring_free, 1)
                    else:
                        c = slice(h * BANK, (h + 1) * BANK)
                        nc.vector.scalar_tensor_tensor(out=qT[x][1][:, c], in0=ps, scalar=bc[:, x, 0:1],
                                                       in1=qT[x][0][:, c].bitcast(F32), op0=ALU.add,
                                                       op1=ALU.subtract).then_inc(ring_free, 1)
                elif kind == "v":
                    b = j[1]
                    nc.vector.tensor_tensor(vr[1][:, 2 * b:2 * b + 2, :].rearrange("p r n -> p (r n)"), ps,
                                            vr[0][:, 2 * b:2 * b + 2, :].rearrange("p r n -> p (r n)").bitcast(F32),
                                            ALU.subtract).then_inc(ring_free, 1)
                else:
                    _, x, half = j
                    c = slice(half * BANK, (half + 1) * BANK)
                    nc.vector.tensor_tensor(oT[x][1][:, c], ps, oT[x][0][:, c].bitcast(F32),
                                            ALU.subtract).then_inc(ring_free, 1)

            def turned(u, s):
                v.wait_ge(pt_hi, u + 1)
                nc.vector.tensor_tensor(pT[1][:, s % 4, :], PS[:, 4, :], pT[0][:, s % 4, :].bitcast(F32),
                                        ALU.subtract).then_inc(pt_lo, 1)

            def body(at, p, first, last, bank0):
                rb = at.pair_ring(p, first)
                hb = at.pair_hi(p, first)
                u0 = at.unit + p * 8
                k = 0
                kh = 0
                for s in range(8):
                    sl = s % 2
                    js = jobs_of(s, first, last)
                    if s == 0:
                        copy_vectors(at, p * 2 + 1, 1)
                    if s == 4:
                        if not last:
                            copy_vectors(at, p * 2 + 2, 0)
                        nc.vector.tensor_scalar(v_cur[:], v_key[:, bass.ds(p * 2, 2), :], 1.0, None,
                                                ALU.mult).then_inc(v_cur_ready, 1)
                    v.wait_ge(score_done, u0 + (c0("score_done") + s + 1))
                    nc.vector.tensor_reduce(nmaxb[:, sl, :], PS[:, 2 * sl:2 * sl + 2, 0:S + 1], AX.X, ALU.max,
                                            negate=True).then_inc(max_done, 1)
                    if not (first and s == 0):
                        turned(u0 + s - 1, (s - 1) % 8)
                    v.wait_ge(exp_done, u0 + (c0("exp_done") + s + 1))
                    nc.vector.reciprocal(rsb[:, sl, :], sumb[:, sl, :]).then_inc(rec_done, 1)
                    for j in js:
                        lo_job(at, j, rb + k, hb + kh, ring_bank(bank0 + k), p)
                        k += 1
                        kh += j[0] in HI

            def norm(at, n_ln, s_col, affine_first):
                ln_stats(v, n_ln * LN_STEPS + c0("ln_step"), 1e-5, n_ln + (c0("ln_sqrt") + 1))
                ln_normalise(v, xnb)

            def affine(at, n, ps, j, col):
                h, dt = TURNS[j]
                v.wait_ge(ring_full, at.ring + n + 1)
                if j >= 2:
                    v.wait_ge(h_ready, at.lns * 4 + (c0("h_ready") + j - 1))
                nc.vector.tensor_scalar(hf[:, j % 2, :], ps, vec[:, bass.ds(col + dt, 1)], vec[:, bass.ds(col + 2 + dt, 1)],
                                        ALU.mult, ALU.add).then_inc(ring_free, 1)

            def affine_lo(at, j):
                h, dt = TURNS[j]
                v.wait_ge(hf_hi, at.lns * 4 + (c0("hf_hi") + j + 1))
                nc.vector.tensor_tensor(h_lo[:, dt, h * BANK:(h + 1) * BANK], hf[:, j % 2, :],
                                        h_hi[:, dt, h * BANK:(h + 1) * BANK].bitcast(F32),
                                        ALU.subtract).then_inc(h_ready, 1)

            def attention(l, a):
                at = At(l, a)
                v.wait_ge(ring_free, at.ring)
                copy_vectors(at, 0, 0)
                norm(at, at.lns, None, None)
                cv = at.vec + (BH * HEADV + 4)
                flat = v_key[:].rearrange("p h c -> p (h c)")
                nc.vector.tensor_tensor(flat[:, 0:BH * (BH + 1):BH + 2], vec[:, bass.ds(cv + BH, BH)], vec[:, bass.ds(cv, BH)],
                                        ALU.subtract).then_inc(vk_step, 1)
                nc.vector.tensor_scalar(v_key[:, :, BH], vec[:, bass.ds(cv, BH)], 1.0, None, ALU.mult).then_inc(vk_step, 1)
                nc.vector.tensor_scalar(bo_cur[:], bo_all[:, bass.ds(l * 2 + a, 1), :].rearrange("p a d -> p (a d)"), 1.0,
                                        None, ALU.mult).then_inc(vk_step, 1)
                par = (c0("ring_full") + a * R_ATT) % NR
                bank = lambda n: ring_bank(par + n)
                lo_job(at, PRO[0], at.ring, at.hi, bank(0), 0)
                lo_job(at, PRO[1], at.ring + 1, at.hi + 1, bank(1), 0)
                col = at.vec + BH * HEADV
                for j in range(5):
                    if j < 4:
                        affine(at, 2 + j, bank(2 + j), j, col)
                    if j >= 1:
                        affine_lo(at, j - 1)
                lo_job(at, PRO[6], at.ring + 6, at.hi + 2, bank(6), 0)
                lo_job(at, PRO[7], at.ring + 7, at.hi + 3, bank(7), 0)
                v.wait_ge(vk_step, (l * 2 + (a + 1)) * 3)
                each_pair(v, at, body)
                turned(at.unit + UA - 1, 7)
                base = at.ring + (R_ATT - len(TAIL))
                par = (c0("ring_full") + a * R_ATT + R_ATT - len(TAIL)) % NR
                for n, j in enumerate(TAIL):
                    lo_job(at, j, base + n, at.hi + H_ATT - 1, ring_bank(par + n), PAIRS)

            with v.Fori(0, 2) as l:
                attention(l, 0)
                attention(l, 1)
                at = At(l, 2)
                cm = l * MLP_W + VEC.at["mlp"]
                v.wait_ge(ring_free, at.ring)
                nc.vector.tensor_scalar(bcm[:], vec[:, bass.ds(cm + 4, FT)], 1.0, None, ALU.mult)
                norm(at, at.lns, None, None)
                par = (c0("ring_full") + 2 * R_ATT) % NR
                for j in range(5):
                    if j < 4:
                        affine(at, j, ring_bank(par + j), j, cm)
                    if j >= 1:
                        affine_lo(at, j - 1)
                mlp_dve(v, ring_from(par), at.ring, 4, l * G_JOBS + c0("g_ready"),
                        l + c0("b2_added"), gb_hi, gb_lo)

    big.close()

    base_out = dict(count)
    with nc.Block() as block:

        @block.sync
        def _(sp):
            sp.dma_start(out.rearrange("(r p) d -> p r d", p=P), X[:]).then_inc(st_done, 16)
            sp.wait_ge(st_done, 16)

    top.close()


def _layout(i):
    import numpy as np

    a = {k: np.ascontiguousarray(np.asarray(v)) for k, v in i.items()}
    f = np.float32

    def dup(w):
        w = w.reshape(-1, 8, 1, 8)
        return np.ascontiguousarray(np.broadcast_to(w, (w.shape[0], 8, 4, 8)).reshape(w.shape[0], 256))

    def cols(x):
        return np.ascontiguousarray(x.reshape(-1, P).T)

    qkv, bqkv = a["L1_xattn_w_qkv"], a["L1_xattn_b_qkv"]
    kv, bkv = a["L1_xattn_w_kv"], a["L1_xattn_b_kv"]
    o = {
        "x": a["x"].reshape(N, D), "ctx": a["ctx_2048"].reshape(N, D),
        "mask0": a["mask_Bx1xSxS2_ff0"].reshape(B, S, S), "ltor": a["mask_1x1xSxS2_fc1"].reshape(S, S),
        "cross": a["mask_Bx1xSxS2_ff1"].reshape(B, S, S),
        "ident": np.eye(P, dtype=f),
        "swq": np.stack([a["L0_xattn_Wq"], qkv[:, 0:256], a["L1_xattn_w_q"]]),
        "swk": np.stack([dup(a["L0_xattn_Wk"]), qkv[:, 256:512], kv[:, 0:256]]),
        "swv": np.stack([dup(a["L0_xattn_Wv"]), qkv[:, 512:768], kv[:, 256:512]]),
        "swv0": a["L0_xattn_Wv"],
        "swo": np.stack([a["L0_xattn_Wo"], a["L1_xattn_w_ao"], a["L1_xattn_w_co"]]),
        "sbo": np.stack([a["L0_xattn_bo"], a["L1_xattn_b_ao"], a["L1_xattn_b_co"]]),
        "gamma": a["L0_xattn_gamma"].reshape(1, D), "beta": a["L0_xattn_beta"].reshape(1, D),
        "s_w1": a["L1_xattn_w1"], "s_w2": a["L1_xattn_w2"], "s_b2": a["L1_xattn_b2"].reshape(1, D),
    }
    sel = np.zeros((16, 2, P), f)
    for w, hd in enumerate((8, 16)):
        for r in range(P):
            sel[r // hd, w, r] = 1
    o["sel"] = sel
    vec = np.zeros((P, VEC.n), f)

    def put(name, c):
        vec[:, VEC.at[name]:VEC.at[name] + c.shape[1]] = c

    put("s0_bq", cols(a["L0_xattn_bq"])), put("s0_bk", cols(dup(a["L0_xattn_bk"][None])[0]))
    put("s0_bv", cols(dup(a["L0_xattn_bv"][None])[0]))
    put("s1_bq", cols(bqkv[0:256])), put("s1_bk", cols(bqkv[256:512])), put("s1_bv", cols(bqkv[512:768]))
    put("s2_bq", cols(a["L1_xattn_b_q"])), put("s2_bk", cols(bkv[0:256])), put("s2_bv", cols(bkv[256:512]))
    for n in ("ln1", "ln2", "ln3"):
        put(f"L1_{n}_s", cols(a[f"L1_xattn_{n}_s"])), put(f"L1_{n}_b", cols(a[f"L1_xattn_{n}_b"]))
    put("L1_b1", cols(a["L1_xattn_b1"]))
    big = [(layer, k) for layer in ("L2", "L3") for k in (1, 2)]
    blocks = []
    for layer, k in big:
        g = lambda n: a[f"{layer}_xattn_{n}"]
        heads = np.stack([cols(g(f"bq{k}")), cols(g(f"bk{k}")), cols(g(f"bias_k{k}").reshape(-1))], 2).reshape(P, -1)
        blocks.append(np.concatenate([heads, cols(g(f"ln{k}_scale")), cols(g(f"ln{k}_offset")), cols(g(f"bv{k}")),
                                      cols(g(f"bias_v{k}").reshape(-1))], 1))
    put("att", np.concatenate(blocks, 1))
    put("mlp", np.concatenate([np.concatenate([cols(a[f"{layer}_xattn_{n}"]) for n in
                                               ("ln_mlp_scale", "ln_mlp_offset", "b_fc1")], 1)
                               for layer in ("L2", "L3")], 1))
    o["vec"] = vec
    for w in ("wq", "wk", "wv", "wo"):
        o[w] = np.stack([a[f"{layer}_xattn_{w}{k}"] for layer, k in big])
    o["bo"] = np.stack([a[f"{layer}_xattn_bo{k}"] for layer, k in big])
    o["w1"] = np.stack([a[f"{layer}_xattn_w_fc1"] for layer in ("L2", "L3")])
    o["w2"] = np.stack([a[f"{layer}_xattn_w_fc2"] for layer in ("L2", "L3")])
    o["b2"] = np.stack([a[f"{layer}_xattn_b_fc2"] for layer in ("L2", "L3")])
    return o


def _build(nc, arrays):
    io = {k: nc.dram_tensor(f"in_{k}", v.shape, mybir.dt.from_np(v.dtype), kind="ExternalInput").ap()
          for k, v in arrays.items()}
    io["out"] = nc.dram_tensor("out", (N, D), F32, kind="ExternalOutput").ap()
    program(nc, io)


def kernel(**inputs):
    import concourse.bacc as _bacc
    from concourse.bass_utils import run_bass_kernel_spmd as _run

    arrays = _layout(inputs)
    nc = _bacc.Bacc("TRN2", target_bir_lowering=False, num_devices=1)
    _build(nc, arrays)
    r = _run(nc, [{f"in_{k}": v for k, v in arrays.items()}], core_ids=[0])
    return r.results[0]["out"].reshape(B, S, D)
```
